# Optimizing a Trainium2 kernel written in Bass

```python
import numpy as np
import jax
import jax.numpy as jnp

def _softmax(x, axis=-1):
    return jax.nn.softmax(x, axis=axis)

def _gelu(x):
    return jax.nn.gelu(x, approximate=True)

def _silu(x):
    return jax.nn.silu(x)

def _sigmoid(x):
    return jax.nn.sigmoid(x)

def _layernorm(x, axis=-1, eps=1e-05):
    m = jnp.mean(x, axis=axis, keepdims=True)
    v = jnp.var(x, axis=axis, keepdims=True)
    return (x - m) / jnp.sqrt(v + eps)

def _scatter_add(tgt, idx, src, axis=0):
    return tgt.at[idx].add(src)

def _segment_sum(src, seg, n):
    return jax.ops.segment_sum(src, seg, n)
kernel_name = 'mk_macaron_d1_jaxref_r8_f7350b'

def setup_inputs(seed: int=0):
    np.random.seed(seed)
    _w = jnp.asarray

    def _L0_attn_setup():
        import jax, jax.numpy as jnp
        import numpy as np
        H = 512
        D = H // 4
        key = jax.random.key(seed)
        k1, k2, k3, k4, k5 = jax.random.split(key, 5)
        x = jax.random.normal(k1, (4, 512, H), dtype=jnp.float32)
        s_in = 1.0 / np.sqrt(H)
        Wqkv = jax.random.normal(k2, (H, 3 * D), dtype=jnp.float32) * s_in
        bqkv = jax.random.normal(k3, (3 * D,), dtype=jnp.float32) * 0.01
        Wo = jax.random.normal(k4, (D, H), dtype=jnp.float32) * (1.0 / np.sqrt(D))
        bo = jax.random.normal(k5, (H,), dtype=jnp.float32) * 0.01
        return {'x': x, 'Wqkv': Wqkv, 'bqkv': bqkv, 'Wo': Wo, 'bo': bo}
    _L0_attn_in = _L0_attn_setup()

    def _L0_ffn_setup():
        import jax, jax.numpy as jnp
        import numpy as np
        HID = 512
        INTER = 1376
        BITS = 4
        PACK = 8
        MAXQ = 15
        GROUP = 128

        def _dequant(qweight, scales, qzeros, g_idx):
            shifts = jnp.arange(PACK, dtype=jnp.uint32) * BITS
            qw = qweight.astype(jnp.uint32)
            w = (qw[:, None, :] >> shifts[None, :, None] & MAXQ).reshape(-1, qweight.shape[1])
            qz = qzeros.astype(jnp.uint32)
            z = ((qz[:, :, None] >> shifts[None, None, :] & MAXQ) + 1).reshape(qzeros.shape[0], -1)
            s = scales[g_idx]
            return (w.astype(scales.dtype) - z[g_idx].astype(scales.dtype)) * s
        key = jax.random.key(seed)
        ks = jax.random.split(key, 16)

        def qw(k, K, N):
            return jax.random.randint(k, (K // PACK, N), 0, 2147483647, dtype=jnp.int32)

        def qz(k, G, N):
            return jax.random.randint(k, (G, N // PACK), 0, 2147483647, dtype=jnp.int32)

        def sc(k, G, N):
            return jax.random.uniform(k, (G, N), jnp.float32, 0.001, 0.01)
        Gk = HID // GROUP
        Gd = INTER // GROUP
        return {'x': jax.random.normal(ks[0], (4, 256, HID), jnp.float32), 'gate_qweight': qw(ks[1], HID, INTER), 'gate_scales': sc(ks[2], Gk, INTER), 'gate_qzeros': qz(ks[3], Gk, INTER), 'gate_g_idx': (jnp.arange(HID) // GROUP).astype(jnp.int32), 'up_qweight': qw(ks[4], HID, INTER), 'up_scales': sc(ks[5], Gk, INTER), 'up_qzeros': qz(ks[6], Gk, INTER), 'up_g_idx': (jnp.arange(HID) // GROUP).astype(jnp.int32), 'down_qweight': qw(ks[7], INTER, HID), 'down_scales': sc(ks[8], Gd, HID), 'down_qzeros': qz(ks[9], Gd, HID), 'down_g_idx': (jnp.arange(INTER) // GROUP).astype(jnp.int32)}
    _L0_ffn_in = _L0_ffn_setup()
    _d = {'L0_attn_x': _L0_attn_in['x'], 'L0_attn_Wqkv': _L0_attn_in['Wqkv'], 'L0_attn_bqkv': _L0_attn_in['bqkv'], 'L0_attn_Wo': _L0_attn_in['Wo'], 'L0_attn_bo': _L0_attn_in['bo'], 'L0_ffn_gate_qweight': _L0_ffn_in['gate_qweight'], 'L0_ffn_gate_scales': _L0_ffn_in['gate_scales'], 'L0_ffn_gate_qzeros': _L0_ffn_in['gate_qzeros'], 'L0_ffn_gate_g_idx': _L0_ffn_in['gate_g_idx'], 'L0_ffn_up_qweight': _L0_ffn_in['up_qweight'], 'L0_ffn_up_scales': _L0_ffn_in['up_scales'], 'L0_ffn_up_qzeros': _L0_ffn_in['up_qzeros'], 'L0_ffn_up_g_idx': _L0_ffn_in['up_g_idx'], 'L0_ffn_down_qweight': _L0_ffn_in['down_qweight'], 'L0_ffn_down_scales': _L0_ffn_in['down_scales'], 'L0_ffn_down_qzeros': _L0_ffn_in['down_qzeros'], 'L0_ffn_down_g_idx': _L0_ffn_in['down_g_idx']}
    _x0 = _d['L0_attn_x']
    _d['L0_attn_x'] = jax.random.normal(jax.random.fold_in(jax.random.key(seed), 1), (2, 1024, 512), dtype=_x0.dtype)
    del _x0
    return _d

def reference(L0_attn_x, L0_attn_Wqkv, L0_attn_bqkv, L0_attn_Wo, L0_attn_bo, L0_ffn_gate_qweight, L0_ffn_gate_scales, L0_ffn_gate_qzeros, L0_ffn_gate_g_idx, L0_ffn_up_qweight, L0_ffn_up_scales, L0_ffn_up_qzeros, L0_ffn_up_g_idx, L0_ffn_down_qweight, L0_ffn_down_scales, L0_ffn_down_qzeros, L0_ffn_down_g_idx):

    def _L0_attn_ref(x, Wqkv, bqkv, Wo, bo):
        import jax, jax.numpy as jnp
        import numpy as np
        H = 512
        D = H // 4
        B, S, C = x.shape
        d = C // 4
        qkv = jnp.einsum('bsc,cf->bsf', x, Wqkv) + bqkv
        qkv = qkv.reshape(B, S, 3, d)
        q, k, v = (qkv[:, :, 0], qkv[:, :, 1], qkv[:, :, 2])
        scale = 1.0 / jnp.sqrt(jnp.float32(d)).astype(x.dtype)
        attn = jnp.einsum('bqd,bkd->bqk', q, k) * scale
        attn = jax.nn.softmax(attn, axis=-1)
        out = jnp.einsum('bqk,bkd->bqd', attn, v)
        return jnp.einsum('bqd,dc->bqc', out, Wo) + bo

    def _L0_ffn_ref(x, gate_qweight, gate_scales, gate_qzeros, gate_g_idx, up_qweight, up_scales, up_qzeros, up_g_idx, down_qweight, down_scales, down_qzeros, down_g_idx):
        import jax, jax.numpy as jnp
        import numpy as np
        HID = 512
        INTER = 1376
        BITS = 4
        PACK = 8
        MAXQ = 15
        GROUP = 128

        def _dequant(qweight, scales, qzeros, g_idx):
            shifts = jnp.arange(PACK, dtype=jnp.uint32) * BITS
            qw = qweight.astype(jnp.uint32)
            w = (qw[:, None, :] >> shifts[None, :, None] & MAXQ).reshape(-1, qweight.shape[1])
            qz = qzeros.astype(jnp.uint32)
            z = ((qz[:, :, None] >> shifts[None, None, :] & MAXQ) + 1).reshape(qzeros.shape[0], -1)
            s = scales[g_idx]
            return (w.astype(scales.dtype) - z[g_idx].astype(scales.dtype)) * s
        Wg = _dequant(gate_qweight, gate_scales, gate_qzeros, gate_g_idx)
        Wu = _dequant(up_qweight, up_scales, up_qzeros, up_g_idx)
        Wd = _dequant(down_qweight, down_scales, down_qzeros, down_g_idx)
        xf = x.reshape(-1, x.shape[-1])
        h = jax.nn.silu(xf @ Wg) * (xf @ Wu)
        out = h @ Wd
        return out.reshape(x.shape[:-1] + (Wd.shape[1],))
    x = L0_attn_x
    x = x + 0.5 * _L0_ffn_ref(_layernorm(x, axis=-1), L0_ffn_gate_qweight, L0_ffn_gate_scales, L0_ffn_gate_qzeros, L0_ffn_gate_g_idx, L0_ffn_up_qweight, L0_ffn_up_scales, L0_ffn_up_qzeros, L0_ffn_up_g_idx, L0_ffn_down_qweight, L0_ffn_down_scales, L0_ffn_down_qzeros, L0_ffn_down_g_idx)
    x = x + _L0_attn_ref(_layernorm(x, axis=-1), L0_attn_Wqkv, L0_attn_bqkv, L0_attn_Wo, L0_attn_bo)
    x = x + 0.5 * _L0_ffn_ref(_layernorm(x, axis=-1), L0_ffn_gate_qweight, L0_ffn_gate_scales, L0_ffn_gate_qzeros, L0_ffn_gate_g_idx, L0_ffn_up_qweight, L0_ffn_up_scales, L0_ffn_up_qzeros, L0_ffn_up_g_idx, L0_ffn_down_qweight, L0_ffn_down_scales, L0_ffn_down_qzeros, L0_ffn_down_g_idx)
    return x

_drawn_inputs = setup_inputs


def setup_inputs(seed=0):
    import zlib

    import numpy as np

    out = dict(_drawn_inputs(seed))
    spreads = {}
    factors = {'L0_attn_bqkv': 6.9, 'L0_attn_bo': 7.613}
    for name, (base, spread) in spreads.items():
        noise = np.random.default_rng([zlib.crc32(name.encode()), seed]).standard_normal(out[name].shape)
        drawn = base * np.exp(spread * noise) if base else spread * noise
        out[name] = jnp.asarray(drawn.astype(out[name].dtype))
    for name, factor in factors.items():
        out[name] = (out[name] * factor).astype(out[name].dtype)
    return out
```

```python
from contextlib import ExitStack

import numpy as np

import concourse.bass as bass
from concourse import mybir

F32 = mybir.dt.float32
F32R = mybir.dt.float32r
BF16 = mybir.dt.bfloat16
I32 = mybir.dt.int32
ALU = mybir.AluOpType
ACT = mybir.ActivationFunctionType
AX_X = mybir.AxisListType.X

P = 128
TOKENS, HID, INTER = 2048, 512, 1376
PACK, BITS, GROUP = 8, 4, 128
ROWS = 512
ROUNDS = TOKENS // ROWS
RT = ROWS // P
KT = HID // P
NT = -(-INTER // P)
GK, GD = HID // GROUP, INTER // GROUP
HEAD = HID // 4
SEQ = 1024
QT = SEQ // P
EPS = 1e-5
SCALE = float(np.float32(1.0) / np.sqrt(np.float32(HEAD)))
PASSES = ((0, 0), (0, 1), (1, 0))

UNITS = 3 * NT
QSLOTS = 6
ITEM_QKV = UNITS
ITEM_O = UNITS + KT
ITEM_FFN = (0, UNITS + KT + 1)
Z_ROW = 32


def width(i):
    return min(P, INTER - i * P)


def macaron(nc, x, w_qkv, b_qkv, w_o, b_o, packed, scales, zeros, g_idx, ident, shifts, groups, out):
    ctx = ExitStack()
    with ctx:
        at = [-(-nc.sbuf_base // 64) * 64]

        def place(name, shape, dtype, offset=None):
            size = int(np.prod(shape[1:])) * (2 if dtype == BF16 else 4)
            t = nc.alloc_sbuf_tensor_at(name, shape, dtype, offset=at[0] if offset is None else offset)
            if offset is None:
                at[0] += -(-size // 32) * 32
            return t

        wgu_at = at[0]
        wgu = place("wgu", [P, NT, 2, 2, KT, P], F32R)
        wd_at = at[0]
        wd = place("wd", [P, NT, 2, HID], F32R)
        xT = place("xT", [P, 2, KT, ROWS], F32R)
        xn = place("xn", [P, RT, HID], F32)
        xres = place("xres", [P, RT, HID], F32)
        hs = place("hs", [P, 2, ROWS], F32)
        hT = place("hT", [P, 2, 2, ROWS], F32R)
        qs_at = at[0]
        qs = place("qs", [P, QSLOTS, KT, P], I32)
        wf = place("wf", [P, 2, KT * P], F32)
        wi = place("wi", [P, KT * P], BF16)
        tab = [place("tab_gate", [P, INTER], BF16), place("tab_up", [P, INTER], BF16), place("tab_down", [P, HID], BF16)]
        oh_gu = place("oh_gu", [P, 2, HID], BF16)
        oh_d = place("oh_d", [P, INTER], BF16)
        idt = place("idt", [P, P], F32)
        shift = place("shift", [P, 1], I32)
        grp = place("grp", [P, 2], F32)
        bqkv = place("bqkv", [P, 3], F32)
        stats = place("stats", [P, RT, 6], F32)
        mv = place("mv", [P, RT, 2], F32)
        rstd = place("rstd", [P, RT], F32)
        mhalf = place("mhalf", [P, RT], F32)
        spare = place("spare", [P, 1], F32)
        assert at[0] <= nc.sbuf_usable_end, at[0]

        tmp_at = wd_at + 5 * 2 * HID * 4
        idx = place("idx", [P, 2 * HID + INTER], I32, tmp_at)
        idf = place("idf", [P, 2 * HID + INTER], F32, tmp_at + 9600)
        cut_at = wd_at + 2 * HID * 4 * 2
        SC = (GK * INTER // P, GK * INTER // P, GD * HID // P)
        NSC = sum(SC)
        sc = place("sc", [P, NSC], F32, cut_at)
        rest = place("rest", [P, NSC], F32, cut_at + 512)
        rest2 = place("rest2", [P, NSC], F32, cut_at + 1024)
        parts = place("parts", [P, 3, NSC], BF16, cut_at + 1536)
        ZP, ZC = 32, (43, 20)
        zq = place("zq", [ZP, sum(ZC)], I32, cut_at + 2304)
        zi = place("zi", [ZP, sum(ZC), PACK], I32, cut_at + 2560)
        zb = place("zb", [ZP, sum(ZC), PACK], BF16, cut_at + 4608)

        wq = place("wq", [P, 2, KT, 3 * HEAD], F32R, qs_at)
        over = [wgu_at + 3 * 2 * 2 * KT * P * 4]

        def place_over(name, shape, dtype):
            t = place(name, shape, dtype, over[0])
            over[0] += int(np.prod(shape[1:])) * 4
            return t

        wo = place_over("wo", [P, 2, HID], F32R)
        bo = place_over("bo", [P, HID], F32)
        qT = place_over("qT", [P, 2, SEQ], F32R)
        kT = place_over("kT", [P, 2, SEQ], F32R)
        vt = place_over("vt", [P, ROWS], F32)
        v = place_over("v", [P, 2, QT, HEAD], F32R)
        pr = place_over("pr", [P, 2, SEQ], F32)
        pT = place_over("pT", [P, 2, 2, QT, 2 * P], F32R)
        oT = place_over("oT", [P, 2, 2, 2 * P], F32R)
        mx = place_over("mx", [P, QT], F32)
        nmx = place_over("nmx", [P, QT], F32)
        sums = place_over("sums", [P, QT], F32)
        rinv = place_over("rinv", [P, QT], F32)
        assert over[0] <= wd_at + NT * 2 * HID * 4

        ps = ctx.enter_context(nc.psum_tensor("ps", [P, 8, 512], F32))
        TURN_BANK = (2, 3, 0, 1)
        Z_BANK, S_BANK, DOWN_BANK = 2, 3, 4
        PT_BANK, PV_BANK, OUT_BANK, VT_BANK = 2, 0, 1, 7

        stream = nc.dram_tensor("stream", [2 * TOKENS, HID], F32, kind="Internal").ap()
        sizes = (GK * INTER, GK * INTER, GD * HID)
        part_dram = [nc.dram_tensor(f"parts_{n}", [3, s], BF16, kind="Internal").ap() for n, s in enumerate(sizes)]
        zero_dram = [nc.dram_tensor(f"zeros_{n}", [s], BF16, kind="Internal").ap() for n, s in enumerate(sizes)]

        def sem(name):
            return ctx.enter_context(nc.semaphore(name))

        d_small, d_scr, d_scw, d_zr, d_zw, d_tab, d_idx, d_xn, d_wf, d_wo, d_bo = (
            sem(n) for n in ("d_small", "d_scr", "d_scw", "d_zr", "d_zw", "d_tab", "d_idx", "d_xn", "d_wf", "d_wo", "d_bo"))
        d_q = [sem(f"d_q{n}") for n in range(QSLOTS)]
        d_res = [sem(f"d_res{n}") for n in range(RT)]
        d_st = [sem(f"d_st{n}") for n in range(RT)]
        s_gate, s_up, s_down, s_turn, s_sz = (sem(n) for n in ("s_gate", "s_up", "s_down", "s_turn", "s_sz"))
        s_qkv, s_vturn, s_score, s_pturn, s_pv, s_proj = (
            sem(n) for n in ("s_qkv", "s_vturn", "s_score", "s_pturn", "s_pv", "s_proj"))
        s_silu, s_hhi, s_xhi, s_whi, s_qkvhi, s_exp, s_phi, s_ohi = (
            sem(n) for n in ("s_silu", "s_hhi", "s_xhi", "s_whi", "s_qkvhi", "s_exp", "s_phi", "s_ohi"))
        s_h, s_hlo, s_xlo, s_sum, s_bn, s_var, s_ln, s_int, s_unp, s_wf, s_tab, s_oh = (
            sem(n) for n in ("s_h", "s_hlo", "s_xlo", "s_sum", "s_bn", "s_var", "s_ln", "s_int", "s_unp", "s_wf", "s_tab", "s_oh"))
        s_qkvlo, s_max, s_nmx, s_plo, s_olo, s_rinv, s_att = (
            sem(n) for n in ("s_qkvlo", "s_max", "s_nmx", "s_plo", "s_olo", "s_rinv", "s_att"))
        s_cst, s_rstd, s_wlo, s_xb = (sem(n) for n in ("s_cst", "s_rstd", "s_wlo", "s_xb"))

        def f32(ap):
            return ap.bitcast(F32)

        def unit(u):
            return u % 3, u // 3

        def unit_view(u, flat):
            m, i = unit(u)
            if m == 2:
                return flat[0:width(i), :]
            return flat.rearrange("p (k c) -> p k c", k=KT)[:, :, 0:width(i)]

        def unit_weights(u, half):
            m, i = unit(u)
            if m == 2:
                return wd[0:width(i), i, half, :]
            return wgu[:, i, half, m, :, 0:width(i)]

        q_count = [0] * QSLOTS
        q_ready = {}
        for n in range(2 * UNITS):
            q_count[n % QSLOTS] += 16 * (1 if n % 3 == 2 else KT)
            q_ready[n] = q_count[n % QSLOTS]

        src_of = (x, stream[TOKENS:2 * TOKENS, :])
        dst_of = (stream[0:TOKENS, :], out)

        def row_tiles(dram, first):
            return dram[bass.ds(first, ROWS), :].rearrange("(r p) c -> p r c", p=P)

        block = ctx.enter_context(nc.Block())

        @block.sync
        def _(sp):
            def load_round(dram, first, t):
                sp.wait_ge(s_turn, KT * t)
                sp.dma_start(xn[:, :, :], row_tiles(dram, first)).then_inc(d_xn, 16)

            def load_residual(dram, first, t, slots=range(RT)):
                for r in slots:
                    row = first + r * P
                    sp.wait_ge(d_st[r], 16 * t)
                    sp.dma_start(xres[:, r, :], dram[bass.ds(row, P), :]).then_inc(d_res[r], 16)

            def load_units(phase, units):
                for u in units:
                    n = UNITS * phase + u
                    m, i = unit(u)
                    s = n % QSLOTS
                    if u >= QSLOTS:
                        sp.wait_ge(s_int, n - QSLOTS + 1)
                    kt = range(1) if m == 2 else range(KT)
                    for k in kt:
                        if m == 2:
                            rows = packed[2][i * 16:i * 16 + width(i) // PACK, :]
                            dst = unit_view(u, qs[:, s, :, :].rearrange("p k c -> p (k c)"))
                        else:
                            rows = packed[m][k * 16:(k + 1) * 16, i * P:i * P + width(i)]
                            dst = qs[:, s, k, 0:width(i)]
                        n_rows, n_cols = rows.shape
                        src = rows.rearrange("r (o c) -> r o c", o=1).to_broadcast([n_rows, PACK, n_cols])
                        sp.dma_start(dst, src).then_inc(d_q[s], 16)

            def store_round(dram, first, f):
                for r in range(RT):
                    row = first + r * P
                    count = RT * f + r + 1
                    if not isinstance(count, int):
                        count = sp.to_reg(count)
                        sp.wait_ge(d_scw, 48)
                    sp.wait_ge(s_sum, count)
                    sp.dma_start(dram[bass.ds(row, P), :], xres[:, r, :]).then_inc(d_st[r], 16)

            col = 0
            for n in range(3):
                c = SC[n]
                sp.dma_start(sc[:, col:col + c], scales[n].rearrange("g n -> (g n)").rearrange("(p c) -> p c", c=c))\
                    .then_inc(d_scr, 16)
                col += c
            half = ZP // 2
            sp.dma_start(zq[0:half, 0:ZC[0]], zeros[0].rearrange("g n -> (g n)").rearrange("(p c) -> p c", c=ZC[0])).then_inc(d_zr, 16)
            sp.dma_start(zq[half:ZP, 0:ZC[0]], zeros[1].rearrange("g n -> (g n)").rearrange("(p c) -> p c", c=ZC[0])).then_inc(d_zr, 16)
            sp.dma_start(zq[:, ZC[0]:sum(ZC)], zeros[2].rearrange("g n -> (g n)").rearrange("(p c) -> p c", c=ZC[1])).then_inc(d_zr, 16)
            sp.dma_start(xn[:, :, :], row_tiles(x, 0)).then_inc(d_xn, 16)
            sp.dma_start(idt[:, :], ident).then_inc(d_small, 16)
            sp.dma_start(shift[:, :], shifts).then_inc(d_small, 16)
            sp.dma_start(grp[:, :], groups).then_inc(d_small, 16)
            sp.dma_start(bqkv[:, :], b_qkv.rearrange("(j p) -> p j", p=P), allow_slow_non_contiguous=True).then_inc(d_small, 16)
            n_idx = Z_ROW + GD
            col = 0
            for g in g_idx:
                n = g.shape[0]
                sp.dma_start(idx[0:n_idx, col:col + n], g.rearrange("(o n) -> o n", o=1).to_broadcast([n_idx, n])).then_inc(d_idx, 16)
                col += n
            load_units(0, range(4))
            sp.wait_ge(s_tab, 5)
            col = 0
            for n in range(3):
                c = SC[n]
                sp.dma_start(part_dram[n].rearrange("j (p c) -> p j c", c=c), parts[:, :, col:col + c]).then_inc(d_scw, 16)
                col += c
            sp.wait_ge(s_tab, 14)
            zbf = zb[:, :, :].rearrange("p c j -> p (c j)")
            n0 = ZC[0] * PACK
            sp.dma_start(zero_dram[0].rearrange("(p c) -> p c", c=n0), zbf[0:half, 0:n0]).then_inc(d_zw, 16)
            sp.dma_start(zero_dram[1].rearrange("(p c) -> p c", c=n0), zbf[half:ZP, 0:n0]).then_inc(d_zw, 16)
            sp.dma_start(zero_dram[2].rearrange("(p c) -> p c", c=ZC[1] * PACK), zbf[:, n0:]).then_inc(d_zw, 16)
            sp.wait_ge(d_scw, 48)
            sp.wait_ge(d_zw, 48)
            for n, g in enumerate((GK, GK, GD)):
                sp.dma_start(tab[n][0:3 * g, :], part_dram[n].rearrange("j (g n) -> (j g) n", g=g)).then_inc(d_tab, 16)
                sp.dma_start(tab[n][Z_ROW:Z_ROW + g, :], zero_dram[n].rearrange("(g n) -> g n", g=g)).then_inc(d_tab, 16)

            def ffn(phase):
                src, dst = (x, stream[TOKENS:2 * TOKENS, :])[phase], (stream[0:TOKENS, :], out)[phase]
                t0, f0 = 8 * phase, 4 * phase
                load_round(src, ROWS, t0 + 1)
                if phase == 0:
                    for r in range(RT):
                        sp.dma_start(xres[:, r, :], src[r * P:(r + 1) * P, :]).then_inc(d_res[r], 16)
                    load_units(0, range(4, UNITS))
                else:
                    load_residual(src, 0, t0)
                    load_units(1, range(QSLOTS, UNITS))
                store_round(dst, 0, f0)
                with sp.Fori(0, ROUNDS - 2) as before:
                    c = before + 1
                    load_round(src, ROWS * (c + 1), t0 + c + 1)
                    load_residual(src, ROWS * c, t0 + c)
                    store_round(dst, ROWS * c, f0 + c)
                c = ROUNDS - 1
                if phase == 0:
                    load_round(stream, 0, t0 + ROUNDS)
                    for k in range(KT):
                        item = ITEM_QKV + k
                        sp.wait_ge(s_wlo, item - 1)
                        sp.dma_start(wf[:, item % 2, 0:3 * HEAD], w_qkv[k * P:(k + 1) * P, :]).then_inc(d_wf, 16)
                        sp.wait_ge(d_wf, 16 * (k + 1))
                load_residual(src, ROWS * c, t0 + c)
                store_round(dst, ROWS * c, f0 + c)

            ffn(0)

            sp.wait_ge(s_down, NT * ROUNDS)
            sp.wait_ge(s_wlo, ITEM_O - 1)
            sp.dma_start(wf[:, ITEM_O % 2, :], w_o).then_inc(d_wo, 16)
            sp.dma_start(bo[:, :], b_o.rearrange("(o n) -> o n", o=1).to_broadcast([P, HID])).then_inc(d_bo, 16)

            with sp.Fori(0, 2) as b:
                t = 4 + 2 * b
                base = 2 * ROWS * b
                load_residual(stream, base, t)
                load_round(stream, base + ROWS, t + 1)
                load_round(stream, base + 2 * ROWS, t + 2)

                def store(j):
                    row = TOKENS + base + j * P
                    sp.wait_ge(s_att, QT * b + j + 1)
                    sp.dma_start(stream[bass.ds(row, P), :], xres[:, j % RT, :]).then_inc(d_st[j % RT], 16)

                store(0)
                for j in range(1, RT):
                    store(j)
                    load_residual(stream, base + ROWS, t + 1, [j - 1])
                load_residual(stream, base + ROWS, t + 1, [RT - 1])
                for j in range(RT, QT):
                    store(j)

            sp.wait_ge(s_qkv, 3 * ROUNDS)
            load_units(1, range(QSLOTS))
            ffn(1)
            for r in range(RT):
                sp.wait_ge(d_st[r], 16 * 3 * ROUNDS)

        @block.tensor
        def _(pe):
            def product(bank_ap, lhs, rhs, first, last):
                for n, (a, b) in enumerate(PASSES):
                    mm = pe.matmul(bank_ap, lhs(a), rhs(b), start=first and n == 0, stop=last and n == 2)
                return mm

            def turn(t, kts):
                for k in kts:
                    for r in range(RT):
                        mm = pe.transpose(ps[:, TURN_BANK[k], r * P:(r + 1) * P], xn[:, r, k * P:(k + 1) * P], idt[:, :])
                    mm.then_inc(s_turn, 1)

            def gate_up(i, m, pair):
                w = width(i)
                for k in range(KT):
                    mm = product(ps[0:w, 2 * pair + m, :], lambda h: wgu[:, i, h, m, k, 0:w], lambda h: xT[:, h, k, :],
                                 k == 0, k == KT - 1)
                mm.then_inc((s_gate, s_up)[m], 1)

            def down(i, n):
                w = width(i)
                pe.wait_ge(s_hlo, n + 1)
                for r in range(RT):
                    mm = product(ps[:, DOWN_BANK + r, :], lambda h: hT[0:w, i % 2, h, r * P:(r + 1) * P],
                                 lambda h: wd[0:w, i, h, :], i == 0, i == NT - 1)
                mm.then_inc(s_down, 1)

            def scales_zeros(phase, u):
                if u >= UNITS:
                    return
                m, i = unit(u)
                w = width(i)
                if u:
                    pe.wait_ge(s_wf, UNITS * phase + u)
                g = (GK, GK, GD)[m]
                for rows, bank in ((slice(Z_ROW, Z_ROW + g), Z_BANK), (slice(0, 3 * g), S_BANK)):
                    if m == 2:
                        mm = pe.matmul(ps[0:w, bank, :], oh_d[rows, i * P:i * P + w], tab[2][rows, :], start=True, stop=True)
                    else:
                        for k in range(KT):
                            mm = pe.matmul(ps[:, bank, k * P:k * P + w], oh_gu[rows, m, k * P:(k + 1) * P],
                                           tab[m][rows, i * P:i * P + w], start=True, stop=True)
                mm.then_inc(s_sz, 1)

            def ffn_round(phase, c, dequant, turn_next):
                f, t, item = 4 * phase + c, 8 * phase + c, ITEM_FFN[phase]
                pe.wait_ge(s_xlo, KT * (t + 1))
                if dequant:
                    if phase == 0:
                        pe.wait_ge(d_tab, 96)
                        pe.wait_ge(s_oh, 4)
                    scales_zeros(phase, 0)
                    scales_zeros(phase, 1)
                for i in range(NT):
                    n = NT * f + i
                    pair = 0 if dequant else i % 2
                    if dequant:
                        pe.wait_ge(s_wlo, item + 3 * i + 1)
                        if i:
                            pe.wait_ge(s_h, n)
                    elif i >= 2:
                        pe.wait_ge(s_h, n - 1)
                    gate_up(i, 0, pair)
                    if dequant:
                        scales_zeros(phase, 2 if i == 0 else 3 * i + 3)
                        pe.wait_ge(s_wlo, item + 3 * i + 2)
                    gate_up(i, 1, pair)
                    if dequant:
                        scales_zeros(phase, 3 if i == 0 else 3 * i + 4)
                    if i == 0:
                        if dequant:
                            scales_zeros(phase, 4)
                            scales_zeros(phase, 5)
                        continue
                    if i == NT - 1:
                        break
                    if i == 1:
                        if not dequant:
                            pe.wait_ge(s_sum, RT * f)
                        elif phase:
                            pe.wait_ge(s_exp, 2 * QT)
                    if dequant:
                        pe.wait_ge(s_wlo, item + 3 * (i - 1) + 3)
                    down(i - 1, n - 1)
                    if dequant:
                        scales_zeros(phase, 3 * i + 5)
                n = NT * f + NT - 1
                if turn_next:
                    pe.wait_ge(s_ln, RT * (t + 2))
                    if dequant:
                        pe.wait_ge(s_wf, UNITS * (phase + 1))
                    else:
                        pe.wait_ge(s_h, n)
                    turn(t + 1, (0, 1))
                if dequant:
                    pe.wait_ge(s_wlo, item + UNITS)
                down(NT - 2, n - 1)
                if turn_next:
                    pe.wait_ge(s_h, n + 1)
                    turn(t + 1, (2, 3))
                down(NT - 1, n)

            def qkv(a, t, phase_b):
                pe.wait_ge(s_xlo, KT * (t + 1))
                for j in range(3):
                    for k in range(KT):
                        mm = product(ps[:, 4 + j, :], lambda h: wq[:, h, k, j * HEAD:(j + 1) * HEAD], lambda h: xT[:, h, k, :],
                                     k == 0, k == KT - 1)
                    mm.then_inc(s_qkv, 1)
                pe.wait_ge(s_ln, RT * (t + 2))
                turn(t + 1, range(KT))
                pe.wait_ge(s_qkvhi, 4 * a + 3)
                for r in range(RT):
                    mm = pe.transpose(ps[:, VT_BANK, r * P:(r + 1) * P], vt[:, r * P:(r + 1) * P], idt[:, :])
                mm.then_inc(s_vturn, 1)

            def score(b, j):
                m = QT * b + j
                if j >= 2:
                    pe.wait_ge(s_exp, m - 1)
                for half in range(2):
                    mm = product(ps[:, 4 + 2 * (j % 2) + half, :], lambda h: qT[:, h, j * P:(j + 1) * P],
                                 lambda h: kT[:, h, half * 512:(half + 1) * 512], True, True)
                mm.then_inc(s_score, 1)

            def turn_p(b, j):
                m = QT * b + j
                pe.wait_ge(s_exp, m + 1)
                for half in range(2):
                    if j:
                        pe.wait_ge(s_plo, 2 * m + half - 1)
                    for k in range(4):
                        c = half * 4 + k
                        mm = pe.transpose(ps[:, PT_BANK + half, k * P:(k + 1) * P], pr[:, j % 2, c * P:(c + 1) * P], idt[:, :])
                    mm.then_inc(s_pturn, 1)

            def pv(b, g):
                pe.wait_ge(s_plo, 2 * QT * b + 4 * g + 4)
                if g:
                    pe.wait_ge(s_olo, 4 * b + g)
                for c in range(QT):
                    mm = product(ps[:, PV_BANK, 0:2 * P], lambda h: v[:, h, c, :], lambda h: pT[:, g % 2, h, c, :],
                                 c == 0, c == QT - 1)
                mm.then_inc(s_pv, 1)

            def project(b, j):
                g = j // 2
                pe.wait_ge(s_olo, 4 * b + g + 1)
                if j:
                    pe.wait_ge(s_att, QT * b + j)
                product(ps[:, OUT_BANK, :], lambda h: oT[:, g % 2, h, (j % 2) * P:(j % 2 + 1) * P],
                        lambda h: wo[:, h, :], True, True).then_inc(s_proj, 1)

            pe.wait_ge(d_small, 64)
            pe.wait_ge(s_ln, RT)
            turn(0, range(KT))
            ffn_round(0, 0, True, True)
            with pe.Fori(1, ROUNDS) as c:
                ffn_round(0, c, False, True)

            pe.wait_ge(s_sum, RT * ROUNDS)
            pe.wait_ge(s_wlo, ITEM_O)
            with pe.Fori(0, 2) as b:
                qkv(2 * b, 4 + 2 * b, b)
                pe.wait_ge(s_qkvlo, 3 * (2 * b + 1))
                qkv(2 * b + 1, 5 + 2 * b, b)
                pe.wait_ge(s_qkvlo, 3 * (2 * b + 2))
                pe.wait_ge(s_xlo, KT * (7 + 2 * b))
                score(b, 0)
                score(b, 1)
                for g in range(QT // 2):
                    turn_p(b, 2 * g)
                    if g < 3:
                        score(b, 2 * g + 2)
                    if g:
                        if g == 1:
                            pe.wait_ge(s_wlo, ITEM_O + 1)
                        project(b, 2 * g - 2)
                    turn_p(b, 2 * g + 1)
                    if g < 3:
                        score(b, 2 * g + 3)
                    if g:
                        project(b, 2 * g - 1)
                    pv(b, g)
                project(b, QT - 2)
                project(b, QT - 1)
                pe.wait_ge(s_att, QT * b + QT)

            ffn_round(1, 0, True, True)
            with pe.Fori(1, ROUNDS - 1) as c:
                ffn_round(1, c, False, True)
            ffn_round(1, ROUNDS - 1, False, False)

        @block.scalar
        def _(act):
            def x_hi(t):
                for k in range(KT):
                    act.wait_ge(s_turn, KT * t + k + 1)
                    act.activation(xT[:, 0, k, :], ps[:, TURN_BANK[k], :], ACT.Copy).then_inc(s_xhi, 1)

            def w_hi(phase, u):
                if u >= UNITS:
                    return
                item = ITEM_FFN[phase] + u
                act.wait_ge(s_wf, UNITS * phase + u + 1)
                act.activation(unit_weights(u, 0), unit_view(u, wf[:, item % 2, :]), ACT.Copy).then_inc(s_whi, 1)

            def ffn_round(phase, c, dequant, turn_next):
                f, t = 4 * phase + c, 8 * phase + c
                if dequant:
                    w_hi(phase, 0)
                    w_hi(phase, 1)
                for i in range(NT):
                    n = NT * f + i
                    w = width(i)
                    pair = 0 if dequant else i % 2
                    act.wait_ge(s_gate, n + 1)
                    if not dequant or phase or i >= 2:
                        act.wait_ge(s_hlo, n - 1)
                    act.activation(hs[0:w, i % 2, :], ps[0:w, 2 * pair, :], ACT.Silu).then_inc(s_silu, 1)
                    if dequant:
                        w_hi(phase, 2 if i == 0 else 3 * i + 3)
                    act.wait_ge(s_h, n + 1)
                    if not dequant or phase or i >= 2:
                        act.wait_ge(s_down, n - 1)
                    act.activation(hT[0:w, i % 2, 0, :], hs[0:w, i % 2, :], ACT.Copy).then_inc(s_hhi, 1)
                    if dequant:
                        w_hi(phase, 3 if i == 0 else 3 * i + 4)
                        if i == 0:
                            w_hi(phase, 4)
                        w_hi(phase, 3 * i + 5)
                if turn_next:
                    x_hi(t + 1)

            x_hi(0)
            ffn_round(0, 0, True, True)
            with act.Fori(1, ROUNDS - 1) as c:
                ffn_round(0, c, False, True)
            for k in range(KT):
                act.wait_ge(d_wf, 16 * (k + 1))
                act.activation(wq[:, 0, k, :], wf[:, (ITEM_QKV + k) % 2, 0:3 * HEAD], ACT.Copy).then_inc(s_whi, 1)
            ffn_round(0, ROUNDS - 1, False, True)
            act.wait_ge(d_wo, 16)
            act.activation(wo[:, 0, :], wf[:, ITEM_O % 2, :], ACT.Copy).then_inc(s_whi, 1)

            def p_hi(b, j):
                m, g = QT * b + j, j // 2
                for half in range(2):
                    act.wait_ge(s_pturn, 2 * m + half + 1)
                    if g >= 2 and j % 2 == 0 and half == 0:
                        act.wait_ge(s_pv, 4 * b + g - 1)
                    act.activation(pT[:, g % 2, 0, 4 * half:4 * half + 4, (j % 2) * P:(j % 2 + 1) * P],
                                   ps[:, PT_BANK + half, :].rearrange("p (k c) -> p k c", k=4), ACT.Copy).then_inc(s_phi, 1)

            def exp(b, j):
                m = QT * b + j
                act.wait_ge(s_nmx, m + 1)
                if j >= 2:
                    act.wait_ge(s_pturn, 2 * m - 2)
                act.activation(pr[:, j % 2, :], ps[:, 4 + 2 * (j % 2):6 + 2 * (j % 2), :].rearrange("p a c -> p (a c)"), ACT.Exp,
                               bias=nmx[:, j:j + 1], scale=SCALE, accum_out=sums[:, j:j + 1]).then_inc(s_exp, 1)

            with act.Fori(0, 2) as b:
                for half in range(2):
                    a = 2 * b + half
                    for j, dst in enumerate((qT, kT)):
                        act.wait_ge(s_qkv, 3 * a + j + 1)
                        act.activation(dst[:, 0, half * ROWS:(half + 1) * ROWS], ps[:, 4 + j, :], ACT.Identity,
                                       bias=bqkv[:, j:j + 1]).then_inc(s_qkvhi, 1)
                    act.wait_ge(s_qkv, 3 * a + 3)
                    act.activation(vt[:, :], ps[:, 6, :], ACT.Identity, bias=bqkv[:, 2:3]).then_inc(s_qkvhi, 1)
                    x_hi(4 + a + 1)
                    act.wait_ge(s_vturn, a + 1)
                    act.activation(v[:, 0, 4 * half:4 * half + 4, :].rearrange("p c d -> p (c d)"), ps[:, VT_BANK, :], ACT.Copy)\
                        .then_inc(s_qkvhi, 1)
                exp(b, 0)
                exp(b, 1)
                for g in range(QT // 2):
                    p_hi(b, 2 * g)
                    if g < 3:
                        exp(b, 2 * g + 2)
                    p_hi(b, 2 * g + 1)
                    if g < 3:
                        exp(b, 2 * g + 3)
                    act.wait_ge(s_pv, 4 * b + g + 1)
                    if g >= 2:
                        act.wait_ge(s_proj, QT * b + 2 * g - 2)
                    act.activation(oT[:, g % 2, 0, :], ps[:, PV_BANK, 0:2 * P], ACT.Copy).then_inc(s_ohi, 1)

            act.wait_ge(s_att, 2 * QT)
            ffn_round(1, 0, True, True)
            with act.Fori(1, ROUNDS - 1) as c:
                ffn_round(1, c, False, True)
            ffn_round(1, ROUNDS - 1, False, False)

        @block.vector
        def _(dve):
            def ln_stats(t, tiles):
                if 0 in tiles:
                    dve.wait_ge(d_xn, 16 * (t + 1))
                for r in tiles:
                    dve.bn_stats(stats[:, r, :], xn[:, r, :]).then_inc(s_bn, 1)

            def ln_var(t):
                dve.wait_ge(s_bn, RT * (t + 1))
                dve.memset(spare[:, :], 0.0)
                for r in range(RT):
                    aggr = dve.bn_aggr(mv[:, r, :], stats[:, r, :])
                aggr.then_inc(s_var, 1)
                dve.wait_ge(s_var, 2 * t + 1)
                dve.tensor_scalar(rstd[:, :], mv[:, :, 1], EPS, None, ALU.add).then_inc(s_var, 1)

            def ln_apply(t, tiles):
                dve.wait_ge(s_rstd, t + 1)
                for r in tiles:
                    dve.tensor_scalar(xn[:, r, :], xn[:, r, :], mv[:, r, 0:1], rstd[:, r:r + 1],
                                      ALU.subtract, ALU.mult).then_inc(s_ln, 1)

            def x_lo(t):
                for k in range(KT):
                    dve.wait_ge(s_xhi, KT * t + k + 1)
                    dve.tensor_tensor(out=xT[:, 1, k, :], in0=ps[:, TURN_BANK[k], :], in1=f32(xT[:, 0, k, :]),
                                      op=ALU.subtract).then_inc(s_xlo, 1)

            def unpack(phase, u):
                if u >= UNITS:
                    return
                n = UNITS * phase + u
                s = n % QSLOTS
                dve.wait_ge(d_q[s], q_ready[n])
                flat = unit_view(u, qs[:, s, :, :].rearrange("p k c -> p (k c)"))
                dve.tensor_scalar(flat, flat, shift[0:flat.shape[0], 0:1], 15, ALU.logical_shift_right,
                                  ALU.bitwise_and).then_inc(s_unp, 1)

            def dequantise(phase, u):
                if u >= UNITS:
                    return
                n, item = UNITS * phase + u, ITEM_FFN[phase] + u
                flat = unit_view(u, qs[:, n % QSLOTS, :, :].rearrange("p k c -> p (k c)"))
                dve.wait_ge(s_unp, n + 1)
                dve.wait_ge(s_sz, n + 1)
                dve.tensor_tensor(out=unit_view(u, wi[:, :]), in0=flat, in1=unit_view(u, ps[:, Z_BANK, :]),
                                  op=ALU.subtract).then_inc(s_int, 1)
                dve.wait_ge(s_int, n + 1)
                if item >= 2:
                    dve.wait_ge(s_wlo, item - 1)
                dve.tensor_tensor(out=unit_view(u, wf[:, item % 2, :]), in0=unit_view(u, wi[:, :]),
                                  in1=unit_view(u, ps[:, S_BANK, :]), op=ALU.mult).then_inc(s_wf, 1)
                unpack(phase, u + 1)

            def ffn_round(phase, c, dequant, turn_next):
                f, t = 4 * phase + c, 8 * phase + c
                if dequant:
                    unpack(phase, 0)
                    dequantise(phase, 0)
                    dequantise(phase, 1)
                for i in range(NT):
                    n = NT * f + i
                    w = width(i)
                    pair = 0 if dequant else i % 2
                    if dequant:
                        dequantise(phase, 2 if i == 0 else 3 * i + 3)
                    dve.wait_ge(s_up, n + 1)
                    dve.wait_ge(s_silu, n + 1)
                    dve.tensor_tensor(out=hs[0:w, i % 2, :], in0=hs[0:w, i % 2, :], in1=ps[0:w, 2 * pair + 1, :],
                                      op=ALU.mult).then_inc(s_h, 1)
                    if dequant:
                        dequantise(phase, 3 if i == 0 else 3 * i + 4)
                    if turn_next:
                        if i in (2, 3):
                            ln_stats(t + 1, (2 * i - 4, 2 * i - 3))
                        if i == 4:
                            ln_var(t + 1)
                        if i in (6, 7):
                            ln_apply(t + 1, (2 * i - 12, 2 * i - 11))
                    dve.wait_ge(s_hhi, n + 1)
                    dve.tensor_tensor(out=hT[0:w, i % 2, 1, :], in0=hs[0:w, i % 2, :], in1=f32(hT[0:w, i % 2, 0, :]),
                                      op=ALU.subtract).then_inc(s_hlo, 1)
                    if dequant:
                        if i == 0:
                            dequantise(phase, 4)
                        dequantise(phase, 3 * i + 5)
                if turn_next:
                    x_lo(t + 1)
                dve.wait_ge(s_down, NT * (f + 1))
                for r in range(RT):
                    dve.wait_ge(d_res[r], 16 * (t + 1))
                    dve.scalar_tensor_tensor(out=xres[:, r, :], in0=ps[:, DOWN_BANK + r, :], scalar=0.5, in1=xres[:, r, :],
                                             op0=ALU.mult, op1=ALU.add).then_inc(s_sum, 1)

            dve.wait_ge(d_scr, 48)
            steps = [0]

            def step(ins):
                ins.then_inc(s_tab, 1)
                steps[0] += 1
                dve.wait_ge(s_tab, steps[0])

            step(dve.tensor_copy(parts[:, 0, :], sc[:, :]))
            step(dve.tensor_tensor(out=rest[:, :], in0=sc[:, :], in1=parts[:, 0, :], op=ALU.subtract))
            step(dve.tensor_copy(parts[:, 1, :], rest[:, :]))
            step(dve.tensor_tensor(out=rest2[:, :], in0=rest[:, :], in1=parts[:, 1, :], op=ALU.subtract))
            step(dve.tensor_copy(parts[:, 2, :], rest2[:, :]))
            dve.wait_ge(d_zr, 48)
            for j in range(PACK):
                step(dve.tensor_scalar(zi[:, :, j], zq[:, :], BITS * j, 15, ALU.logical_shift_right, ALU.bitwise_and))
            step(dve.tensor_scalar(zb[:, :, :].rearrange("p c j -> p (c j)"), zi[:, :, :].rearrange("p c j -> p (c j)"),
                                   1.0, None, ALU.add))
            ln_stats(0, range(RT))
            ln_var(0)

            dve.wait_ge(d_idx, 48)
            dve.wait_ge(d_small, 64)
            rows = Z_ROW + GD
            done = [0]

            def one_hot(cols, n_groups, which, dst):
                src, tmp = idx[0:rows, cols], idf[0:rows, cols]
                g = float(n_groups)
                for make in (
                    lambda: dve.tensor_scalar(tmp, src, 0.0, g, ALU.is_lt, ALU.mult),
                    lambda: dve.tensor_tensor(out=tmp, in0=tmp, in1=src, op=ALU.add),
                    lambda: dve.tensor_scalar(tmp, tmp, g - 1.0, 0.0, ALU.min, ALU.max),
                    lambda: dve.tensor_scalar(dst, tmp, grp[0:rows, which:which + 1], None, ALU.is_equal),
                ):
                    make().then_inc(s_oh, 1)
                    done[0] += 1
                    dve.wait_ge(s_oh, done[0])

            one_hot(slice(0, 2 * HID), GK, 0, oh_gu[0:rows, :, :].rearrange("p m n -> p (m n)"))
            ln_apply(0, range(RT))
            one_hot(slice(2 * HID, 2 * HID + INTER), GD, 1, oh_d[0:rows, :])
            x_lo(0)
            ffn_round(0, 0, True, True)
            with dve.Fori(1, ROUNDS) as c:
                ffn_round(0, c, False, True)

            def maximum(b, j):
                m = QT * b + j
                dve.wait_ge(s_score, m + 1)
                dve.reduce_max(mx[:, j:j + 1], ps[:, 4 + 2 * (j % 2):6 + 2 * (j % 2), :].rearrange("p a c -> p (a c)"), AX_X)\
                    .then_inc(s_max, 1)
                dve.wait_ge(s_max, m + 1)
                dve.tensor_scalar(nmx[:, j:j + 1], mx[:, j:j + 1], -SCALE, None, ALU.mult).then_inc(s_nmx, 1)

            def p_lo(b, j):
                m, g = QT * b + j, j // 2
                for half in range(2):
                    dve.wait_ge(s_phi, 2 * m + half + 1)
                    at_ = (slice(4 * half, 4 * half + 4), slice((j % 2) * P, (j % 2 + 1) * P))
                    dve.tensor_tensor(out=pT[:, g % 2, 1, at_[0], at_[1]],
                                      in0=ps[:, PT_BANK + half, :].rearrange("p (k c) -> p k c", k=4),
                                      in1=f32(pT[:, g % 2, 0, at_[0], at_[1]]), op=ALU.subtract).then_inc(s_plo, 1)

            def total(b, j):
                m = QT * b + j
                dve.wait_ge(s_exp, m + 1)
                dve.reciprocal(rinv[:, j:j + 1], sums[:, j:j + 1]).then_inc(s_rinv, 1)
                dve.wait_ge(s_rinv, m + 1)
                dve.wait_ge(s_proj, m + 1)
                dve.wait_ge(s_xb, m + 1)
                dve.scalar_tensor_tensor(out=xres[:, j % RT, :], in0=ps[:, OUT_BANK, :], scalar=rinv[:, j:j + 1],
                                         in1=xres[:, j % RT, :], op0=ALU.mult, op1=ALU.add).then_inc(s_att, 1)

            with dve.Fori(0, 2) as b:
                for half in range(2):
                    a = 2 * b + half
                    t = 4 + a
                    for j, dst in enumerate((qT, kT)):
                        dve.wait_ge(s_qkvhi, 4 * a + j + 1)
                        cols = slice(half * ROWS, (half + 1) * ROWS)
                        dve.scalar_tensor_tensor(out=dst[:, 1, cols], in0=ps[:, 4 + j, :], scalar=bqkv[:, j:j + 1],
                                                 in1=f32(dst[:, 0, cols]), op0=ALU.add, op1=ALU.subtract).then_inc(s_qkvlo, 1)
                    ln_stats(t + 1, range(RT))
                    ln_var(t + 1)
                    ln_apply(t + 1, range(RT))
                    x_lo(t + 1)
                    dve.wait_ge(s_qkvhi, 4 * a + 4)
                    rows_ = slice(4 * half, 4 * half + 4)
                    dve.tensor_tensor(out=v[:, 1, rows_, :].rearrange("p c d -> p (c d)"), in0=ps[:, VT_BANK, :],
                                      in1=f32(v[:, 0, rows_, :]).rearrange("p c d -> p (c d)"), op=ALU.subtract)\
                        .then_inc(s_qkvlo, 1)
                maximum(b, 0)
                maximum(b, 1)
                for g in range(QT // 2):
                    p_lo(b, 2 * g)
                    if g < 3:
                        maximum(b, 2 * g + 2)
                    if g:
                        total(b, 2 * g - 2)
                    p_lo(b, 2 * g + 1)
                    if g < 3:
                        maximum(b, 2 * g + 3)
                    if g:
                        total(b, 2 * g - 1)
                    dve.wait_ge(s_ohi, 4 * b + g + 1)
                    dve.tensor_tensor(out=oT[:, g % 2, 1, :], in0=ps[:, PV_BANK, 0:2 * P], in1=f32(oT[:, g % 2, 0, :]),
                                      op=ALU.subtract).then_inc(s_olo, 1)
                total(b, QT - 2)
                total(b, QT - 1)

            ffn_round(1, 0, True, True)
            with dve.Fori(1, ROUNDS - 1) as c:
                ffn_round(1, c, False, True)
            ffn_round(1, ROUNDS - 1, False, False)

        @block.gpsimd
        def _(pool):
            def deviation(t):
                pool.wait_ge(s_var, 2 * (t + 1))
                pool.tensor_tensor(out=rstd[:, :], in0=rstd[:, :], in1=mhalf[:, :], op=ALU.pow).then_inc(s_rstd, 1)

            def w_lo(phase, u):
                if u >= UNITS:
                    return
                item = ITEM_FFN[phase] + u
                pool.wait_ge(s_whi, item + 1)
                pool.tensor_tensor(out=unit_weights(u, 1), in0=unit_view(u, wf[:, item % 2, :]),
                                   in1=f32(unit_weights(u, 0)), op=ALU.subtract).then_inc(s_wlo, 1)

            pool.memset(mhalf[:, :], -0.5).then_inc(s_cst, 1)
            pool.wait_ge(s_cst, 1)
            deviation(0)

            def ffn(phase):
                for u in range(UNITS):
                    if u == 16:
                        deviation(8 * phase + 1)
                    w_lo(phase, u)
                with pool.Fori(1, ROUNDS - 1) as c:
                    deviation(8 * phase + 1 + c)

            ffn(0)
            for k in range(KT):
                pool.wait_ge(s_whi, ITEM_QKV + k + 1)
                pool.tensor_tensor(out=wq[:, 1, k, :], in0=wf[:, (ITEM_QKV + k) % 2, 0:3 * HEAD], in1=f32(wq[:, 0, k, :]),
                                   op=ALU.subtract).then_inc(s_wlo, 1)
            deviation(4)
            pool.wait_ge(s_whi, ITEM_O + 1)
            pool.tensor_tensor(out=wo[:, 1, :], in0=wf[:, ITEM_O % 2, :], in1=f32(wo[:, 0, :]), op=ALU.subtract).then_inc(s_wlo, 1)
            pool.wait_ge(d_bo, 16)
            with pool.Fori(0, 2) as b:
                def add_bias(k):
                    for r in range(RT):
                        pool.wait_ge(d_res[r], 16 * (4 + 2 * b + k + 1))
                        pool.tensor_tensor(out=xres[:, r, :], in0=xres[:, r, :], in1=bo[:, :], op=ALU.add).then_inc(s_xb, 1)
                deviation(5 + 2 * b)
                deviation(6 + 2 * b)
                add_bias(0)
                add_bias(1)
            ffn(1)


def kernel(**inputs):
    import concourse.bacc as bacc
    from concourse.bass_utils import run_bass_kernel_spmd

    nc = bacc.Bacc("TRN2", target_bir_lowering=False, num_devices=1)
    arrays = {}

    def take(name, a):
        a = np.ascontiguousarray(a)
        arrays[name] = a
        return nc.dram_tensor(name, a.shape, mybir.dt.from_np(a.dtype), kind="ExternalInput").ap()

    src = {k: take(f"in_{k}", np.asarray(v)) for k, v in inputs.items()}
    ident = take("in_ident", np.eye(P, dtype=np.float32))
    shifts = take("in_shifts", (BITS * (np.arange(P) % PACK)).astype(np.int32)[:, None])
    rows = np.arange(P)
    groups = take("in_groups", np.stack([rows % GK, np.where(rows < Z_ROW, rows % GD, rows - Z_ROW)], 1).astype(np.float32))
    out = nc.dram_tensor("out_0", (TOKENS, HID), F32, kind="ExternalOutput").ap()
    mats = ("gate", "up", "down")
    macaron(nc, src["L0_attn_x"].rearrange("b s c -> (b s) c"), src["L0_attn_Wqkv"], src["L0_attn_bqkv"],
            src["L0_attn_Wo"], src["L0_attn_bo"], [src[f"L0_ffn_{m}_qweight"] for m in mats],
            [src[f"L0_ffn_{m}_scales"] for m in mats], [src[f"L0_ffn_{m}_qzeros"] for m in mats],
            [src[f"L0_ffn_{m}_g_idx"] for m in mats], ident, shifts, groups, out)
    r = run_bass_kernel_spmd(nc, [arrays], core_ids=[0])
    return r.results[0]["out_0"].reshape(inputs["L0_attn_x"].shape)
```

```python
from contextlib import ExitStack

import numpy as np

import concourse.bass as bass
from concourse import mybir

F32 = mybir.dt.float32
F32R = mybir.dt.float32r
BF16 = mybir.dt.bfloat16
I32 = mybir.dt.int32
ALU = mybir.AluOpType
ACT = mybir.ActivationFunctionType
AX_X = mybir.AxisListType.X

P = 128
TOKENS, HID, INTER = 2048, 512, 1376
PACK, BITS, GROUP = 8, 4, 128
ROWS = 512
ROUNDS = TOKENS // ROWS
RT = ROWS // P
KT = HID // P
NT = -(-INTER // P)
GK, GD = HID // GROUP, INTER // GROUP
HEAD = HID // 4
SEQ = 1024
QT = SEQ // P
EPS = 1e-5
SCALE = float(np.float32(1.0) / np.sqrt(np.float32(HEAD)))
PASSES = ((0, 0), (0, 1), (1, 0))

UNITS = 3 * NT
QSLOTS = 6
ITEM_QKV = UNITS
ITEM_O = UNITS + KT
ITEM_FFN = (0, UNITS + KT + 1)
Z_ROW = 32
FOLD = 64
D_TILES = 6
D_COLS = D_TILES * P
D_FROM = INTER - D_COLS


def width(i):
    return min(P, INTER - i * P)


def macaron(nc, x, w_qkv, b_qkv, w_o, b_o, packed, scales, zeros, g_idx, ident, shifts, groups, out):
    ctx = ExitStack()
    with ctx:
        at = [-(-nc.sbuf_base // 64) * 64]

        def place(name, shape, dtype, offset=None):
            size = int(np.prod(shape[1:])) * (2 if dtype == BF16 else 4)
            t = nc.alloc_sbuf_tensor_at(name, shape, dtype, offset=at[0] if offset is None else offset)
            if offset is None:
                at[0] += -(-size // 32) * 32
            return t

        wgu_at = at[0]
        wgu = place("wgu", [P, NT, 2, 2, KT, P], F32R)
        wd_at = at[0]
        wd = place("wd", [P, NT, 2, HID], F32R)
        xT = place("xT", [P, 2, KT, ROWS], F32R)
        xn = place("xn", [P, RT, HID], F32)
        xres = place("xres", [P, RT, HID], F32)
        hs = place("hs", [P, 2, ROWS], F32)
        hT = place("hT", [P, 2, 2, ROWS], F32R)
        qs_at = at[0]
        qs = place("qs", [P, QSLOTS, KT, P], I32)
        wf = place("wf", [P, 2, KT * P], F32)
        wi = place("wi", [P, KT * P], BF16)
        tab_gu = place("tab_gu", [P, INTER], BF16)
        tab_d = place("tab_d", [P, HID], BF16)
        oh_gu = place("oh_gu", [P, HID], BF16)
        oh_d = place("oh_d", [P, D_COLS], BF16)
        idt = place("idt", [P, P], F32)
        shift = place("shift", [P, 1], I32)
        grp = place("grp", [P, 4], F32)
        bqkv = place("bqkv", [P, 3], F32)
        stats = place("stats", [P, RT, 6], F32)
        mv = place("mv", [P, RT, 2], F32)
        rstd = place("rstd", [P, RT], F32)
        mhalf = place("mhalf", [P, RT], F32)
        spare = place("spare", [P, 1], F32)
        assert at[0] <= nc.sbuf_usable_end, at[0]

        tmp_at = wd_at + 5 * 2 * HID * 4
        idx = place("idx", [P, HID + D_COLS], I32, tmp_at)
        idf = place("idf", [P, HID + D_COLS], F32, tmp_at + (HID + D_COLS) * 4)
        free = [wd_at + 2 * 2 * HID * 4]

        def scratch(name, shape, dtype):
            t = place(name, shape, dtype, free[0])
            free[0] += -(-int(np.prod(shape[1:])) * (2 if dtype == BF16 else 4) // 32) * 32
            return t

        SC = GK * INTER // P
        ZP = 16
        ZC = GK * INTER // PACK // ZP
        SP_D, SC_D = 8 * GD, HID // 8
        ZP_D, ZC_D = 4 * GD, HID // PACK // 4
        cuts = []
        for kind, n_p, n_c, z_p, z_c in (("gu", P, 2 * SC, 2 * ZP, ZC), ("d", SP_D, SC_D, ZP_D, ZC_D)):
            cuts.append((
                scratch(f"sc_{kind}", [P, n_c], F32)[0:n_p, :],
                scratch(f"rest_{kind}", [P, n_c], F32)[0:n_p, :],
                scratch(f"rest2_{kind}", [P, n_c], F32)[0:n_p, :],
                scratch(f"parts_{kind}", [P, 3, n_c], BF16)[0:n_p, :, :],
                scratch(f"zq_{kind}", [P, z_c], I32)[0:z_p, :],
                scratch(f"zi_{kind}", [P, z_c, PACK], I32)[0:z_p, :, :],
                scratch(f"zb_{kind}", [P, z_c, PACK], BF16)[0:z_p, :, :]))
        assert free[0] <= tmp_at

        wq = place("wq", [P, 2, KT, 3 * HEAD], F32R, qs_at)
        over = [wgu_at + 3 * 2 * 2 * KT * P * 4]

        def place_over(name, shape, dtype):
            t = place(name, shape, dtype, over[0])
            over[0] += int(np.prod(shape[1:])) * 4
            return t

        xn_odd = place_over("xn_odd", [P, RT, HID], F32)
        wo = place_over("wo", [P, 2, HID], F32R)
        bo = place_over("bo", [P, HID], F32)
        qT = place_over("qT", [P, 2, SEQ], F32R)
        kT = place_over("kT", [P, 2, SEQ], F32R)
        vt = place_over("vt", [P, ROWS], F32)
        v = place_over("v", [P, 2, QT, HEAD], F32R)
        pr = place_over("pr", [P, 2, SEQ], F32)
        pT = place_over("pT", [P, 2, 2, QT, 2 * P], F32R)
        oT = place_over("oT", [P, 2, 2, 2 * P], F32R)
        xT_odd = place_over("xT_odd", [P, 2, KT, ROWS], F32R)
        osb = place_over("osb", [P, 2, HID], F32)
        mx = place_over("mx", [P, QT], F32)
        nmx = place_over("nmx", [P, QT], F32)
        sums = place_over("sums", [P, QT], F32)
        rinv = place_over("rinv", [P, QT], F32)
        assert over[0] <= wd_at + NT * 2 * HID * 4

        def x_rows(t):
            return xn_odd if isinstance(t, int) and t in (5, 7) else xn

        def x_turned(t):
            return xT_odd if isinstance(t, int) and t in (5, 7) else xT

        XN_LOADS = {6: 5, 7: 2, 8: 6}

        ps = ctx.enter_context(nc.psum_tensor("ps", [P, 8, 512], F32))
        TURN_BANK = (2, 3, 0, 1)
        Z_BANK, S_BANK, DOWN_BANK = 2, 3, 4

        def pair_of(dequant, i):
            return i % 2 if not dequant else 0 if i else 2

        def turn_bank(t, k):
            return 4 + k if isinstance(t, int) and t == 0 else TURN_BANK[k]

        PT_BANK, PV_BANK, OUT_BANK = 2, 0, 1
        Q_BANK, K_BANK, V_BANK, VT_BANK = (5, 1), (6, 4), (4, 0), (7, 0)
        QKV_ORDER = ((2, 0, 1), (1, 2, 0))

        stream = nc.dram_tensor("stream", [2 * TOKENS, HID], F32, kind="Internal").ap()

        def sem(name):
            return ctx.enter_context(nc.semaphore(name))

        d_small, d_grp, d_cut_gu, d_cut_d, d_idx_gu, d_idx_d, d_xn, d_xn_odd, d_bqkv, d_wo, d_bo = (
            sem(n) for n in ("d_small", "d_grp", "d_cut_gu", "d_cut_d", "d_idx_gu", "d_idx_d", "d_xn", "d_xn_odd", "d_bqkv", "d_wo", "d_bo"))
        d_q = [sem(f"d_q{n}") for n in range(QSLOTS)]
        d_tab = [sem(f"d_tab{n}") for n in range(4)]
        d_wf = [sem(f"d_wf{n}") for n in range(2)]
        d_x0 = [sem(f"d_x0{n}") for n in range(RT)]
        d_res = [sem(f"d_res{n}") for n in range(RT)]
        d_st = [sem(f"d_st{n}") for n in range(RT)]
        s_gate, s_up, s_down, s_rows, s_turn, s_sz = (
            sem(n) for n in ("s_gate", "s_up", "s_down", "s_rows", "s_turn", "s_sz"))
        s_qkv, s_vturn, s_score, s_pturn, s_pv, s_proj = (
            sem(n) for n in ("s_qkv", "s_vturn", "s_score", "s_pturn", "s_pv", "s_proj"))
        s_silu, s_hhi, s_xhi, s_whi, s_qkvhi, s_exp, s_phi, s_ohi, s_out = (
            sem(n) for n in ("s_silu", "s_hhi", "s_xhi", "s_whi", "s_qkvhi", "s_exp", "s_phi", "s_ohi", "s_out"))
        s_h, s_hlo, s_xlo, s_sum, s_bn, s_var, s_ln, s_int, s_unp, s_wf, s_tab, s_oh = (
            sem(n) for n in ("s_h", "s_hlo", "s_xlo", "s_sum", "s_bn", "s_var", "s_ln", "s_int", "s_unp", "s_wf", "s_tab", "s_oh"))
        s_qkvlo, s_max, s_nmx, s_plo, s_olo, s_rinv, s_last = (
            sem(n) for n in ("s_qkvlo", "s_max", "s_nmx", "s_plo", "s_olo", "s_rinv", "s_last"))
        s_cst, s_cut, s_ohd, s_rstd, s_wlo, s_xb, s_att = (
            sem(n) for n in ("s_cst", "s_cut", "s_ohd", "s_rstd", "s_wlo", "s_xb", "s_att"))

        def by_dve(b, j):
            return b == 1 and j >= QT - 2

        def out_bank(b, j):
            return DOWN_BANK + 2 + j % 2 if by_dve(b, j) else OUT_BANK

        def f32(ap):
            return ap.bitcast(F32)

        def unit(u):
            return u % 3, u // 3

        def unit_view(u, flat):
            m, i = unit(u)
            if m == 2:
                return flat[0:width(i), :]
            return flat.rearrange("p (k c) -> p k c", k=KT)[:, :, 0:width(i)]

        def unit_weights(u, half):
            m, i = unit(u)
            if m == 2:
                return wd[0:width(i), i, half, :]
            return wgu[:, i, half, m, :, 0:width(i)]

        q_count = [0] * QSLOTS
        q_ready = {}
        for n in range(2 * UNITS):
            q_count[n % QSLOTS] += 16 * (1 if n % 3 == 2 else KT)
            q_ready[n] = q_count[n % QSLOTS]

        src_of = (x, stream[TOKENS:2 * TOKENS, :])
        dst_of = (stream[0:TOKENS, :], out)

        def row_tiles(dram, first):
            return dram[bass.ds(first, ROWS), :].rearrange("(r p) c -> p r c", p=P)

        def flat(ap, n_cols):
            return ap.rearrange("g n -> (g n)").rearrange("(p c) -> p c", c=n_cols)

        def spread(indices):
            return indices.rearrange("(o n) -> o n", o=1).to_broadcast([FOLD, indices.shape[0]])

        def table(eng, m, at_row=0):
            if m == 2:
                (_, _, _, parts, _, _, zb), dst, g, done = cuts[1], tab_d, GD, d_tab[3 if at_row else 2]
            else:
                (_, _, _, parts, _, _, zb), dst, g, done, at_row = cuts[0], tab_gu, GK, d_tab[m], FOLD * m
                parts, zb = parts[:, :, m * SC:(m + 1) * SC], zb[m * ZP:(m + 1) * ZP, :, :]
            for j in range(3):
                eng.dma_start(dst[at_row + j * g:at_row + (j + 1) * g, :], parts[:, j, :]).then_inc(done, 16)
            row = at_row + Z_ROW
            eng.dma_start(dst[row:row + g, :], zb.rearrange("p c j -> p (c j)")).then_inc(done, 16)

        def maker(eng, semaphore):
            made = [0]

            def step(*instructions):
                for make in instructions:
                    make().then_inc(semaphore, 1)
                    made[0] += 1
                eng.wait_ge(semaphore, made[0])
            return step

        CUT_STEPS, ZERO_STEPS = 5, PACK + 1

        def cut_scales(eng, step, sc, rest, rest2, parts, zq, zi, zb):
            step(lambda: eng.tensor_copy(parts[:, 0, :], sc))
            step(lambda: eng.tensor_tensor(out=rest, in0=sc, in1=parts[:, 0, :], op=ALU.subtract))
            step(lambda: eng.tensor_copy(parts[:, 1, :], rest))
            step(lambda: eng.tensor_tensor(out=rest2, in0=rest, in1=parts[:, 1, :], op=ALU.subtract))
            step(lambda: eng.tensor_copy(parts[:, 2, :], rest2))

        def unpack_zeros(eng, step, sc, rest, rest2, parts, zq, zi, zb):
            step(*(lambda j=j: eng.tensor_scalar(zi[:, :, j], zq, BITS * j, 15, ALU.logical_shift_right, ALU.bitwise_and)
                   for j in range(PACK)))
            step(lambda: eng.tensor_scalar(zb.rearrange("p c j -> p (c j)"), zi.rearrange("p c j -> p (c j)"),
                                           1.0, None, ALU.add))

        def clamp_and_compare(eng, step, cols, n_groups, which, dst):
            step(lambda: eng.tensor_scalar(idf[:, cols], idx[:, cols], -float(n_groups), n_groups - 1.0, ALU.max, ALU.min))
            step(lambda: eng.tensor_scalar(dst, idf[:, cols], grp[:, which + 2:which + 3], None, ALU.is_equal))

        def one_hot(eng, step, cols, which, dst):
            step(lambda: eng.scalar_tensor_tensor(out=dst, in0=idf[:, cols], scalar=grp[:, which:which + 1], in1=dst,
                                                  op0=ALU.is_equal, op1=ALU.add))

        GU_COLS, DOWN_COLS = slice(0, HID), slice(HID, HID + D_COLS)

        block = ctx.enter_context(nc.Block())

        @block.sync
        def _(sp):
            def load_round(dram, first, t):
                odd = x_rows(t) is xn_odd
                sp.wait_ge(s_turn, KT * (t - (1 if odd or t in (6, 8) else 0)) if isinstance(t, int) else KT * t)
                sp.dma_start(x_rows(t)[:, :, :], row_tiles(dram, first)).then_inc(d_xn_odd if odd else d_xn, 16)

            def load_residual(dram, first, t, slots=range(RT)):
                for r in slots:
                    row = first + r * P
                    sp.wait_ge(d_st[r], 16 * t)
                    sp.dma_start(xres[:, r, :], dram[bass.ds(row, P), :]).then_inc(d_res[r], 16)

            def load_units(phase, units):
                for u in units:
                    n = UNITS * phase + u
                    m, i = unit(u)
                    s = n % QSLOTS
                    if u >= QSLOTS:
                        sp.wait_ge(s_int, n - QSLOTS + 1)
                    kt = range(1) if m == 2 else range(KT)
                    for k in kt:
                        if m == 2:
                            rows = packed[2][i * 16:i * 16 + width(i) // PACK, :]
                            dst = unit_view(u, qs[:, s, :, :].rearrange("p k c -> p (k c)"))
                        else:
                            rows = packed[m][k * 16:(k + 1) * 16, i * P:i * P + width(i)]
                            dst = qs[:, s, k, 0:width(i)]
                        n_rows, n_cols = rows.shape
                        src = rows.rearrange("r (o c) -> r o c", o=1).to_broadcast([n_rows, PACK, n_cols])
                        sp.dma_start(dst, src).then_inc(d_q[s], 16)

            def store_round(dram, first, f):
                for r in range(RT):
                    row = first + r * P
                    count = RT * f + r + 1
                    if not isinstance(count, int):
                        count = sp.to_reg(count)
                        sp.wait_ge(s_tab, 5)
                    sp.wait_ge(s_sum, count)
                    sp.dma_start(dram[bass.ds(row, P), :], xres[:, r, :]).then_inc(d_st[r], 16)

            (sc_gu, _, _, _, zq_gu, _, _), _ = cuts
            for m in range(2):
                sp.dma_start(sc_gu[:, m * SC:(m + 1) * SC], flat(scales[m], SC)).then_inc(d_cut_gu, 16)
            for m in range(2):
                sp.dma_start(zq_gu[m * ZP:(m + 1) * ZP, :], flat(zeros[m], ZC)).then_inc(d_cut_gu, 16)
            sp.dma_start(grp[:, :], groups).then_inc(d_grp, 16)
            sp.dma_start(idt[:, :], ident).then_inc(d_small, 16)
            sp.dma_start(shift[:, :], shifts).then_inc(d_small, 16)
            load_units(0, [0])
            sp.wait_ge(s_cut, CUT_STEPS)
            sp.wait_ge(s_tab, ZERO_STEPS)
            table(sp, 1)
            load_units(0, [1, 2])
            sp.wait_ge(s_cut, 2 * CUT_STEPS)
            sp.wait_ge(s_tab, 2 * ZERO_STEPS)
            table(sp, 2)
            load_units(0, [3, 4, 5])
            table(sp, 2, FOLD)
            sp.dma_start(bqkv[:, :], b_qkv.rearrange("(j p) -> p j", p=P), allow_slow_non_contiguous=True).then_inc(d_bqkv, 16)

            def ffn(phase):
                src, dst = (x, stream[TOKENS:2 * TOKENS, :])[phase], (stream[0:TOKENS, :], out)[phase]
                t0, f0 = 8 * phase, 4 * phase
                if phase == 0:
                    load_units(0, range(QSLOTS, QSLOTS + 3))
                    load_round(src, ROWS, t0 + 1)
                    load_units(0, range(QSLOTS + 3, 2 * QSLOTS))
                    for r in range(RT):
                        sp.dma_start(xres[:, r, :], src[r * P:(r + 1) * P, :]).then_inc(d_res[r], 16)
                    load_units(0, range(2 * QSLOTS, UNITS))
                else:
                    load_round(src, ROWS, t0 + 1)
                    load_residual(src, 0, t0)
                    load_units(1, range(QSLOTS, UNITS))
                store_round(dst, 0, f0)
                with sp.Fori(0, ROUNDS - 2) as before:
                    c = before + 1
                    load_round(src, ROWS * (c + 1), t0 + c + 1)
                    load_residual(src, ROWS * c, t0 + c)
                    store_round(dst, ROWS * c, f0 + c)
                c = ROUNDS - 1
                if phase == 0:
                    load_round(stream, 0, t0 + ROUNDS)
                load_residual(src, ROWS * c, t0 + c)
                if phase == 0:
                    for k in range(KT):
                        item = ITEM_QKV + k
                        sp.wait_ge(s_wlo, item - 1)
                        sp.dma_start(wf[:, item % 2, 0:3 * HEAD], w_qkv[k * P:(k + 1) * P, :]).then_inc(d_wf[item % 2], 16)
                    sp.wait_ge(s_up, NT * c + 4)
                    load_round(stream, ROWS, 5)
                    load_round(stream, 2 * ROWS, 6)
                    sp.wait_ge(s_up, NT * c + 6)
                    sp.wait_ge(s_wlo, ITEM_O - 1)
                    sp.dma_start(wf[:, ITEM_O % 2, :], w_o).then_inc(d_wo, 16)
                    sp.dma_start(bo[:, :], b_o.rearrange("(o n) -> o n", o=1).to_broadcast([P, HID])).then_inc(d_bo, 16)
                store_round(dst, ROWS * c, f0 + c)

            ffn(0)

            for b in range(2):
                t = 4 + 2 * b
                base = 2 * ROWS * b
                load_residual(stream, base, t)
                if b == 0:
                    load_round(stream, base + 3 * ROWS, t + 3)
                else:
                    sp.wait_ge(s_qkv, 3 * ROUNDS)
                    load_units(1, range(QSLOTS))

                def store(j):
                    if by_dve(b, j):
                        sp.wait_ge(s_last, j - QT + 3)
                    else:
                        sp.wait_ge(s_att, QT * b + j + 1)
                    row = TOKENS + base + j * P
                    sp.dma_start(stream[row:row + P, :], xres[:, j % RT, :]).then_inc(d_st[j % RT], 16)

                store(0)
                for j in range(1, RT):
                    store(j)
                    load_residual(stream, base + ROWS, t + 1, [j - 1])
                load_residual(stream, base + ROWS, t + 1, [RT - 1])
                if b == 0:
                    load_round(stream, TOKENS, t + 4)
                for j in range(RT, QT):
                    store(j)

            ffn(1)
            for r in range(RT):
                sp.wait_ge(d_st[r], 16 * 3 * ROUNDS)

        @block.tensor
        def _(pe):
            def product(bank_ap, lhs, rhs, first, last):
                for n, (a, b) in enumerate(PASSES):
                    mm = pe.matmul(bank_ap, lhs(a), rhs(b), start=first and n == 0, stop=last and n == 2)
                return mm

            def turn(t, kts):
                for k in kts:
                    for r in range(RT):
                        mm = pe.transpose(ps[:, turn_bank(t, k), r * P:(r + 1) * P], x_rows(t)[:, r, k * P:(k + 1) * P],
                                          idt[:, :])
                    mm.then_inc(s_turn, 1)

            def gate_up(i, m, pair, kts=range(KT), by_tile=False):
                w = width(i)
                for k in kts:
                    if by_tile:
                        pe.wait_ge(s_xlo, k + 1)
                    mm = product(ps[0:w, 2 * pair + m, :], lambda h: wgu[:, i, h, m, k, 0:w], lambda h: xT[:, h, k, :],
                                 k == 0, k == KT - 1)
                if k == KT - 1:
                    mm.then_inc((s_gate, s_up)[m], 1)

            def down(i, n):
                w = width(i)
                pe.wait_ge(s_hlo, n + 1)
                for r in range(RT):
                    mm = product(ps[:, DOWN_BANK + r, :], lambda h: hT[0:w, i % 2, h, r * P:(r + 1) * P],
                                 lambda h: wd[0:w, i, h, :], i == 0, i == NT - 1)
                    if i == NT - 1 and r < RT - 1:
                        mm.then_inc(s_rows, 1)
                mm.then_inc(s_down, 1)

            def scales_zeros(phase, u):
                if u >= UNITS:
                    return
                m, i = unit(u)
                w = width(i)
                if u:
                    if phase == 0 and u in (2, 3 * D_TILES + 2):
                        if u == 2:
                            pe.wait_ge(s_oh, 4)
                        pe.wait_ge(d_tab[2 if u == 2 else 3], 64)
                    pe.wait_ge(s_wf, UNITS * phase + u)
                g = (GK, GK, GD)[m]
                row = FOLD if m == 1 or (m == 2 and i >= D_TILES) else 0
                for rows, bank in ((slice(row + Z_ROW, row + Z_ROW + g), Z_BANK), (slice(row, row + 3 * g), S_BANK)):
                    if m == 2:
                        col = i * P - (D_FROM if row else 0)
                        mm = pe.matmul(ps[0:w, bank, :], oh_d[rows, col:col + w], tab_d[rows, :], start=True, stop=True)
                    else:
                        for k in range(KT):
                            mm = pe.matmul(ps[:, bank, k * P:k * P + w], oh_gu[rows, k * P:(k + 1) * P],
                                           tab_gu[rows, i * P:i * P + w], start=True, stop=True)
                mm.then_inc(s_sz, 1)

            def ffn_round(phase, c, dequant, turn_next):
                f, t, item = 4 * phase + c, 8 * phase + c, ITEM_FFN[phase]
                if not dequant or phase:
                    pe.wait_ge(s_xlo, KT * (t + 1))
                for i in range(NT):
                    n = NT * f + i
                    pair = pair_of(dequant, i)
                    if dequant:
                        pe.wait_ge(s_wlo, item + 3 * i + 1)
                        if i >= 2:
                            pe.wait_ge(s_h, n)
                    elif i >= 2:
                        pe.wait_ge(s_h, n - 1)
                    if dequant and i == 0:
                        gate_up(0, 0, pair, (0, 1), by_tile=phase == 0)
                        if phase:
                            scales_zeros(phase, 2)
                        gate_up(0, 0, pair, (2, 3), by_tile=phase == 0)
                        scales_zeros(phase, 3 if phase else 2)
                        pe.wait_ge(s_wlo, item + 2)
                        gate_up(0, 1, pair, (0, 1))
                        scales_zeros(phase, 4 if phase else 3)
                        gate_up(0, 1, pair, (2, 3))
                        if phase == 0:
                            scales_zeros(phase, 4)
                        continue
                    if dequant and i == 1:
                        gate_up(i, 0, pair, (0, 1))
                        scales_zeros(phase, 5)
                        gate_up(i, 0, pair, (2, 3))
                    else:
                        gate_up(i, 0, pair)
                    if dequant:
                        scales_zeros(phase, 3 * i + 3)
                        pe.wait_ge(s_wlo, item + 3 * i + 2)
                    gate_up(i, 1, pair)
                    if dequant:
                        scales_zeros(phase, 3 * i + 4)
                    if i == 0:
                        continue
                    if i == NT - 1:
                        break
                    if i == 1:
                        if not dequant:
                            pe.wait_ge(s_sum, RT * f)
                        elif phase:
                            pe.wait_ge(s_last, 2)
                    if dequant:
                        pe.wait_ge(s_wlo, item + 3 * (i - 1) + 3)
                    down(i - 1, n - 1)
                    if dequant:
                        scales_zeros(phase, 3 * i + 5)
                n = NT * f + NT - 1
                if turn_next:
                    pe.wait_ge(s_ln, RT * (t + 2))
                    if dequant:
                        pe.wait_ge(s_wf, UNITS * (phase + 1))
                    else:
                        pe.wait_ge(s_h, n)
                    turn(t + 1, (0, 1))
                if dequant:
                    pe.wait_ge(s_wlo, item + UNITS)
                down(NT - 2, n - 1)
                if turn_next:
                    pe.wait_ge(s_h, n + 1)
                    turn(t + 1, (2, 3))
                down(NT - 1, n)

            def qkv_product(a, j):
                half = a % 2
                src = x_turned(4 + a)
                for k in range(KT):
                    if j == QKV_ORDER[half][0]:
                        pe.wait_ge(s_xlo, KT * (4 + a) + k + 1)
                    mm = product(ps[:, (Q_BANK, K_BANK, V_BANK)[j][half], :], lambda h: wq[:, h, k, j * HEAD:(j + 1) * HEAD],
                                 lambda h: src[:, h, k, :], k == 0, k == KT - 1)
                mm.then_inc(s_qkv, 1)

            def turn_v(a):
                pe.wait_ge(s_qkvhi, 4 * a + (2 if a % 2 else 1))
                for r in range(RT):
                    mm = pe.transpose(ps[:, VT_BANK[a % 2], r * P:(r + 1) * P], vt[:, r * P:(r + 1) * P], idt[:, :])
                mm.then_inc(s_vturn, 1)

            def qkv_first(a):
                t = 4 + a
                if a == 0:
                    pe.wait_ge(s_ln, RT * (t + 2))
                    pe.wait_ge(s_xlo, KT * (t + 1))
                    turn(t + 1, range(KT))
                    pe.wait_ge(s_sum, RT * ROUNDS - 3)
                    pe.wait_ge(s_wlo, ITEM_O)
                    qkv_product(a, 2)
                    pe.wait_ge(s_sum, RT * ROUNDS)
                qkv_product(a, 0)
                qkv_product(a, 1)
                if a:
                    pe.wait_ge(s_out, QT)
                    turn(t + 1, (2, 3))
                turn_v(a)

            def qkv_second(a):
                t, b = 4 + a, a // 2
                pe.wait_ge(s_qkvhi, 4 * (a - 1) + 1)
                qkv_product(a, 1)
                pe.wait_ge(s_ln, RT * (t + 2))
                turn(t + 1, range(KT))
                pe.wait_ge(s_qkvlo, 3 * a + 1)
                score(b, 0)
                score(b, 1)
                pe.wait_ge(s_xlo, KT * (t + 1) + 3)
                qkv_product(a, 2)
                turn_p(b, 0)
                pe.wait_ge(s_xlo, KT * (t + 1) + 4)
                qkv_product(a, 0)
                turn_p(b, 1)
                turn_v(a)

            def score(b, j):
                m = QT * b + j
                if j >= 2:
                    pe.wait_ge(s_exp, m - 1)
                for half in range(2):
                    mm = product(ps[:, 4 + 2 * (j % 2) + half, :], lambda h: qT[:, h, j * P:(j + 1) * P],
                                 lambda h: kT[:, h, half * 512:(half + 1) * 512], True, True)
                mm.then_inc(s_score, 1)

            def turn_p(b, j):
                m = QT * b + j
                pe.wait_ge(s_exp, m + 1)
                for half in range(2):
                    if j:
                        pe.wait_ge(s_plo, 2 * m + half - 1)
                    for k in range(4):
                        c = half * 4 + k
                        mm = pe.transpose(ps[:, PT_BANK + half, k * P:(k + 1) * P], pr[:, j % 2, c * P:(c + 1) * P], idt[:, :])
                    mm.then_inc(s_pturn, 1)

            def pv(b, g):
                pe.wait_ge(s_plo, 2 * QT * b + 4 * g + 4)
                if g:
                    pe.wait_ge(s_olo, 4 * b + g)
                for c in range(QT):
                    mm = product(ps[:, PV_BANK, 0:2 * P], lambda h: v[:, h, c, :], lambda h: pT[:, g % 2, h, c, :],
                                 c == 0, c == QT - 1)
                mm.then_inc(s_pv, 1)

            def project(b, j):
                g = j // 2
                pe.wait_ge(s_olo, 4 * b + g + 1)
                if j and not by_dve(b, j):
                    pe.wait_ge(s_out, QT * b + j)
                product(ps[:, out_bank(b, j), :], lambda h: oT[:, g % 2, h, (j % 2) * P:(j % 2 + 1) * P],
                        lambda h: wo[:, h, :], True, True).then_inc(s_proj, 1)

            def keep_warm(n):
                for _ in range(n):
                    pe.matmul(ps[:, 1, 0:P], idt[:, :], idt[:, :], start=True, stop=True)

            pe.wait_ge(d_small, 32)
            keep_warm(10)
            for r in range(RT):
                pe.wait_ge(s_ln, r + 1)
                for k in range(KT):
                    mm = pe.transpose(ps[:, turn_bank(0, k), r * P:(r + 1) * P], xn[:, r, k * P:(k + 1) * P], idt[:, :])
                    if r == RT - 1:
                        mm.then_inc(s_turn, 1)
            pe.wait_ge(d_tab[0], 64)
            pe.wait_ge(s_oh, 3)
            scales_zeros(0, 0)
            keep_warm(6)
            pe.wait_ge(d_tab[1], 64)
            scales_zeros(0, 1)
            keep_warm(6)
            ffn_round(0, 0, True, True)
            with pe.Fori(1, ROUNDS) as c:
                ffn_round(0, c, False, True)

            for b in range(2):
                qkv_first(2 * b)
                qkv_second(2 * b + 1)
                for g in range(QT // 2):
                    for j in (2 * g, 2 * g + 1):
                        if g:
                            turn_p(b, j)
                            if j == 2:
                                pe.wait_ge(s_wlo, ITEM_O + 1)
                            project(b, j - 2)
                        if g < 3:
                            score(b, j + 2)
                    if g == 0:
                        pe.wait_ge(s_qkvlo, 3 * (2 * b + 2))
                    if b and g == 3:
                        pe.wait_ge(s_plo, 4 * QT)
                        scales_zeros(1, 0)
                    if b == 0 and g == 3:
                        pe.wait_ge(s_exp, QT)
                        qkv_product(2, 2)
                    pv(b, g)
                if b:
                    scales_zeros(1, 1)
                else:
                    pe.wait_ge(s_ln, RT * 8)
                    turn(7, (0, 1))
                project(b, QT - 2)
                project(b, QT - 1)
            pe.wait_ge(s_out, 2 * QT - 2)

            ffn_round(1, 0, True, True)
            with pe.Fori(1, ROUNDS - 1) as c:
                ffn_round(1, c, False, True)
            ffn_round(1, ROUNDS - 1, False, False)

        @block.scalar
        def _(act):
            def x_hi(t, kts=range(KT)):
                for k in kts:
                    act.wait_ge(s_turn, KT * t + k + 1)
                    act.activation(x_turned(t)[:, 0, k, :], ps[:, turn_bank(t, k), :], ACT.Copy).then_inc(s_xhi, 1)

            def w_hi(phase, u):
                if u >= UNITS:
                    return
                item = ITEM_FFN[phase] + u
                act.wait_ge(s_wf, UNITS * phase + u + 1)
                act.activation(unit_weights(u, 0), unit_view(u, wf[:, item % 2, :]), ACT.Copy).then_inc(s_whi, 1)

            def ffn_round(phase, c, dequant, turn_next, last_of_first=False):
                f, t = 4 * phase + c, 8 * phase + c
                if dequant and phase == 0:
                    w_hi(phase, 1)
                for i in range(NT):
                    n = NT * f + i
                    w = width(i)
                    pair = pair_of(dequant, i)
                    act.wait_ge(s_gate, n + 1)
                    if not dequant or phase or i >= 2:
                        act.wait_ge(s_hlo, n - 1)
                    act.activation(hs[0:w, i % 2, :], ps[0:w, 2 * pair, :], ACT.Silu).then_inc(s_silu, 1)
                    if dequant:
                        if phase and i == 2:
                            act.wait_ge(s_last, 2)
                        for u in (2, 3) if i == 0 else (3 * i + 3,):
                            w_hi(phase, u)
                    act.wait_ge(s_h, n + 1)
                    if not dequant or phase or i >= 2:
                        act.wait_ge(s_down, n - 1)
                    act.activation(hT[0:w, i % 2, 0, :], hs[0:w, i % 2, :], ACT.Copy).then_inc(s_hhi, 1)
                    if dequant:
                        w_hi(phase, 3 * i + 4)
                        w_hi(phase, 3 * i + 5)
                    if last_of_first and 1 <= i <= KT:
                        slot = (ITEM_QKV + i - 1) % 2
                        act.wait_ge(d_wf[slot], 16 * ((i + 1) // 2))
                        act.activation(wq[:, 0, i - 1, :], wf[:, slot, 0:3 * HEAD], ACT.Copy).then_inc(s_whi, 1)
                if turn_next:
                    x_hi(t + 1)

            for r in range(RT):
                act.dma_start(xn[:, r, :], x[r * P:(r + 1) * P, :]).then_inc(d_x0[r], 16)
            for m in range(2):
                act.dma_start(idx[FOLD * m:FOLD * m + FOLD, GU_COLS], spread(g_idx[m])).then_inc(d_idx_gu, 16)
            act.wait_ge(s_cut, CUT_STEPS)
            act.wait_ge(s_tab, ZERO_STEPS)
            table(act, 0)
            x_hi(0)
            w_hi(0, 0)
            ffn_round(0, 0, True, True)
            with act.Fori(1, ROUNDS - 1) as c:
                ffn_round(0, c, False, True)
            ffn_round(0, ROUNDS - 1, False, True, last_of_first=True)
            act.wait_ge(d_bqkv, 16)
            act.wait_ge(d_wo, 16)
            act.activation(wo[:, 0, :], wf[:, ITEM_O % 2, :], ACT.Copy).then_inc(s_whi, 1)

            def p_hi(b, j):
                m, g = QT * b + j, j // 2
                for half in range(2):
                    act.wait_ge(s_pturn, 2 * m + half + 1)
                    if g >= 2 and j % 2 == 0 and half == 0:
                        act.wait_ge(s_pv, 4 * b + g - 1)
                    act.activation(pT[:, g % 2, 0, 4 * half:4 * half + 4, (j % 2) * P:(j % 2 + 1) * P],
                                   ps[:, PT_BANK + half, :].rearrange("p (k c) -> p k c", k=4), ACT.Copy).then_inc(s_phi, 1)

            def exp(b, j):
                m = QT * b + j
                act.wait_ge(s_nmx, m + 1)
                if j >= 2:
                    act.wait_ge(s_pturn, 2 * m - 2)
                act.activation(pr[:, j % 2, :], ps[:, 4 + 2 * (j % 2):6 + 2 * (j % 2), :].rearrange("p a c -> p (a c)"), ACT.Exp,
                               bias=nmx[:, j:j + 1], scale=SCALE, accum_out=sums[:, j:j + 1]).then_inc(s_exp, 1)

            def scaled(b, j):
                m = QT * b + j
                act.wait_ge(s_rinv, m + 1)
                act.wait_ge(s_proj, m + 1)
                if m >= 2:
                    act.wait_ge(s_att, m - 1)
                act.activation(osb[:, j % 2, :], ps[:, OUT_BANK, :], ACT.Copy, scale=rinv[:, j:j + 1]).then_inc(s_out, 1)

            def v_bias(a):
                act.wait_ge(s_qkv, 3 * a + (2 if a % 2 else 1))
                act.activation(vt[:, :], ps[:, V_BANK[a % 2], :], ACT.Identity, bias=bqkv[:, 2:3]).then_inc(s_qkvhi, 1)

            def qk_hi(a, j, dst):
                half = a % 2
                act.wait_ge(s_qkv, 3 * a + QKV_ORDER[half].index(j) + 1)
                act.activation(dst[:, 0, half * ROWS:(half + 1) * ROWS], ps[:, (Q_BANK, K_BANK)[j][half], :], ACT.Identity,
                               bias=bqkv[:, j:j + 1]).then_inc(s_qkvhi, 1)

            def v_hi(a):
                half = a % 2
                act.wait_ge(s_vturn, a + 1)
                act.activation(v[:, 0, 4 * half:4 * half + 4, :].rearrange("p c d -> p (c d)"), ps[:, VT_BANK[half], :], ACT.Copy)\
                    .then_inc(s_qkvhi, 1)

            for b in range(2):
                a = 2 * b
                if b == 0:
                    x_hi(5)
                    v_bias(0)
                qk_hi(a, 0, qT)
                qk_hi(a, 1, kT)
                if b:
                    x_hi(5 + a, (2, 3))
                v_hi(a)
                a = 2 * b + 1
                qk_hi(a, 1, kT)
                x_hi(5 + a)
                exp(b, 0)
                exp(b, 1)
                v_bias(a)
                p_hi(b, 0)
                qk_hi(a, 0, qT)
                p_hi(b, 1)
                v_hi(a)
                for g in range(QT // 2):
                    for j in (2 * g, 2 * g + 1):
                        if g:
                            p_hi(b, j)
                            scaled(b, j - 2)
                    if g < 3:
                        exp(b, 2 * g + 2)
                        exp(b, 2 * g + 3)
                    if g == 3:
                        if b:
                            w_hi(1, 0)
                        else:
                            v_bias(2)
                    act.wait_ge(s_pv, 4 * b + g + 1)
                    if g >= 2:
                        act.wait_ge(s_proj, QT * b + 2 * g - 2)
                    act.activation(oT[:, g % 2, 0, :], ps[:, PV_BANK, 0:2 * P], ACT.Copy).then_inc(s_ohi, 1)
                if b:
                    w_hi(1, 1)
                else:
                    x_hi(7, (0, 1))
                    scaled(b, QT - 2)
                    scaled(b, QT - 1)

            ffn_round(1, 0, True, True)
            with act.Fori(1, ROUNDS - 1) as c:
                ffn_round(1, c, False, True)
            ffn_round(1, ROUNDS - 1, False, False)

        @block.vector
        def _(dve):
            def ln_stats(t, tiles, n_load=None):
                if n_load is not None:
                    dve.wait_ge(d_xn_odd if x_rows(t) is xn_odd else d_xn, 16 * n_load)
                for r in tiles:
                    if isinstance(t, int) and t == 0:
                        dve.wait_ge(d_x0[r], 16)
                    dve.bn_stats(stats[:, r, :], x_rows(t)[:, r, :]).then_inc(s_bn, 1)

            def ln_var(t):
                dve.wait_ge(s_bn, RT * (t + 1))
                dve.memset(spare[:, :], 0.0)
                for r in range(RT):
                    aggr = dve.bn_aggr(mv[:, r, :], stats[:, r, :])
                aggr.then_inc(s_var, 1)
                dve.wait_ge(s_var, 2 * t + 1)
                dve.tensor_scalar(rstd[:, :], mv[:, :, 1], EPS, None, ALU.add).then_inc(s_var, 1)

            def ln_apply(t, tiles):
                dve.wait_ge(s_rstd, t + 1)
                for r in tiles:
                    dve.tensor_scalar(x_rows(t)[:, r, :], x_rows(t)[:, r, :], mv[:, r, 0:1], rstd[:, r:r + 1],
                                      ALU.subtract, ALU.mult).then_inc(s_ln, 1)

            def x_lo(t, kts=range(KT)):
                dst = x_turned(t)
                for k in kts:
                    dve.wait_ge(s_xhi, KT * t + k + 1)
                    dve.tensor_tensor(out=dst[:, 1, k, :], in0=ps[:, turn_bank(t, k), :], in1=f32(dst[:, 0, k, :]),
                                      op=ALU.subtract).then_inc(s_xlo, 1)

            def unpack(phase, u):
                if u >= UNITS:
                    return
                n = UNITS * phase + u
                s = n % QSLOTS
                dve.wait_ge(d_q[s], q_ready[n])
                flat = unit_view(u, qs[:, s, :, :].rearrange("p k c -> p (k c)"))
                dve.tensor_scalar(flat, flat, shift[0:flat.shape[0], 0:1], 15, ALU.logical_shift_right,
                                  ALU.bitwise_and).then_inc(s_unp, 1)

            def dequantise(phase, u, unpack_next=True):
                if u >= UNITS:
                    return
                n, item = UNITS * phase + u, ITEM_FFN[phase] + u
                flat = unit_view(u, qs[:, n % QSLOTS, :, :].rearrange("p k c -> p (k c)"))
                dve.wait_ge(s_unp, n + 1)
                dve.wait_ge(s_sz, n + 1)
                dve.tensor_tensor(out=unit_view(u, wi[:, :]), in0=flat, in1=unit_view(u, ps[:, Z_BANK, :]),
                                  op=ALU.subtract).then_inc(s_int, 1)
                dve.wait_ge(s_int, n + 1)
                if item >= 2:
                    dve.wait_ge(s_wlo, item - 1)
                dve.tensor_tensor(out=unit_view(u, wf[:, item % 2, :]), in0=unit_view(u, wi[:, :]),
                                  in1=unit_view(u, ps[:, S_BANK, :]), op=ALU.mult).then_inc(s_wf, 1)
                if unpack_next:
                    unpack(phase, u + 1)

            def ffn_round(phase, c, dequant, turn_next, last_of_first=False):
                f, t = 4 * phase + c, 8 * phase + c
                if dequant and phase == 0:
                    dequantise(phase, 1)
                    dve.wait_ge(s_ohd, 2)
                    one_hot(dve, compare, DOWN_COLS, 1, oh_d[:, :])
                for i in range(NT):
                    n = NT * f + i
                    w = width(i)
                    pair = pair_of(dequant, i)
                    if dequant:
                        for u in (2, 3, 4) if i == 0 else (3 * i + 3,):
                            dequantise(phase, u)
                            if phase and u == 2:
                                total(1, QT - 2)
                                total(1, QT - 1)
                    dve.wait_ge(s_up, n + 1)
                    dve.wait_ge(s_silu, n + 1)
                    dve.tensor_tensor(out=hs[0:w, i % 2, :], in0=hs[0:w, i % 2, :], in1=ps[0:w, 2 * pair + 1, :],
                                      op=ALU.mult).then_inc(s_h, 1)
                    if dequant and i:
                        dequantise(phase, 3 * i + 4)
                    if turn_next:
                        if i in (2, 3):
                            ln_stats(t + 1, (2 * i - 4, 2 * i - 3), (c + 1 if phase == 0 else c + 7) if i == 2 else None)
                        if i == 4:
                            ln_var(t + 1)
                        if i in (5, 6):
                            ln_apply(t + 1, (2 * i - 10, 2 * i - 9))
                    if last_of_first:
                        if i in (7, 8):
                            ln_stats(5, (2 * i - 14, 2 * i - 13), 1 if i == 7 else None)
                        if i == 9:
                            ln_var(5)
                        if i == 10:
                            ln_apply(5, range(RT))
                    dve.wait_ge(s_hhi, n + 1)
                    dve.tensor_tensor(out=hT[0:w, i % 2, 1, :], in0=hs[0:w, i % 2, :], in1=f32(hT[0:w, i % 2, 0, :]),
                                      op=ALU.subtract).then_inc(s_hlo, 1)
                    if dequant:
                        dequantise(phase, 3 * i + 5)
                if turn_next:
                    x_lo(t + 1)
                for r in range(RT):
                    if r < RT - 1:
                        dve.wait_ge(s_rows, (RT - 1) * f + r + 1)
                    else:
                        dve.wait_ge(s_down, NT * (f + 1))
                    dve.wait_ge(d_res[r], 16 * (t + 1))
                    dve.scalar_tensor_tensor(out=xres[:, r, :], in0=ps[:, DOWN_BANK + r, :], scalar=0.5, in1=xres[:, r, :],
                                             op0=ALU.mult, op1=ALU.add).then_inc(s_sum, 1)

            dve.wait_ge(d_cut_gu, 64)
            tables = maker(dve, s_tab)
            unpack_zeros(dve, tables, *cuts[0])
            ln_stats(0, range(RT))
            ln_var(0)
            dve.wait_ge(d_grp, 16)
            dve.wait_ge(d_idx_gu, 32)
            compare = maker(dve, s_oh)
            clamp_and_compare(dve, compare, GU_COLS, GK, 0, oh_gu[:, :])
            one_hot(dve, compare, GU_COLS, 0, oh_gu[:, :])
            ln_apply(0, range(RT))
            dve.wait_ge(d_small, 32)
            unpack(0, 0)
            dve.wait_ge(d_cut_d, 32)
            unpack_zeros(dve, tables, *cuts[1])
            dequantise(0, 0, unpack_next=False)
            x_lo(0)
            unpack(0, 1)
            ffn_round(0, 0, True, True)
            with dve.Fori(1, ROUNDS - 1) as c:
                ffn_round(0, c, False, True)
            ffn_round(0, ROUNDS - 1, False, True, last_of_first=True)

            def maximum(b, j):
                m = QT * b + j
                dve.wait_ge(s_score, m + 1)
                dve.reduce_max(mx[:, j:j + 1], ps[:, 4 + 2 * (j % 2):6 + 2 * (j % 2), :].rearrange("p a c -> p (a c)"), AX_X)\
                    .then_inc(s_max, 1)
                dve.wait_ge(s_max, m + 1)
                dve.tensor_scalar(nmx[:, j:j + 1], mx[:, j:j + 1], -SCALE, None, ALU.mult).then_inc(s_nmx, 1)

            def p_lo(b, j):
                m, g = QT * b + j, j // 2
                for half in range(2):
                    dve.wait_ge(s_phi, 2 * m + half + 1)
                    at_ = (slice(4 * half, 4 * half + 4), slice((j % 2) * P, (j % 2 + 1) * P))
                    dve.tensor_tensor(out=pT[:, g % 2, 1, at_[0], at_[1]],
                                      in0=ps[:, PT_BANK + half, :].rearrange("p (k c) -> p k c", k=4),
                                      in1=f32(pT[:, g % 2, 0, at_[0], at_[1]]), op=ALU.subtract).then_inc(s_plo, 1)

            def inverse(b, j):
                dve.wait_ge(s_exp, QT * b + j + 1)
                dve.reciprocal(rinv[:, j:j + 1], sums[:, j:j + 1]).then_inc(s_rinv, 1)

            def total(b, j):
                m = QT * b + j
                dve.wait_ge(s_rinv, m + 1)
                dve.wait_ge(s_proj, m + 1)
                dve.wait_ge(s_xb, m + 1)
                dve.scalar_tensor_tensor(out=xres[:, j % RT, :], in0=ps[:, out_bank(b, j), :], scalar=rinv[:, j:j + 1],
                                         in1=xres[:, j % RT, :], op0=ALU.mult, op1=ALU.add).then_inc(s_last, 1)

            def qk_lo(a, j, dst):
                half = a % 2
                dve.wait_ge(s_qkvhi, 4 * a + QKV_ORDER[half].index(j) + 1)
                cols = slice(half * ROWS, (half + 1) * ROWS)
                dve.scalar_tensor_tensor(out=dst[:, 1, cols], in0=ps[:, (Q_BANK, K_BANK)[j][half], :], scalar=bqkv[:, j:j + 1],
                                         in1=f32(dst[:, 0, cols]), op0=ALU.add, op1=ALU.subtract).then_inc(s_qkvlo, 1)

            def v_lo(a):
                half = a % 2
                dve.wait_ge(s_qkvhi, 4 * a + 4)
                rows_ = slice(4 * half, 4 * half + 4)
                dve.tensor_tensor(out=v[:, 1, rows_, :].rearrange("p c d -> p (c d)"), in0=ps[:, VT_BANK[half], :],
                                  in1=f32(v[:, 0, rows_, :]).rearrange("p c d -> p (c d)"), op=ALU.subtract)\
                    .then_inc(s_qkvlo, 1)

            for b in range(2):
                a, t = 2 * b, 6 + 2 * b
                if b == 0:
                    x_lo(5)
                ln_stats(t, range(RT), XN_LOADS[t])
                ln_var(t)
                qk_lo(a, 0, qT)
                ln_apply(t, range(RT))
                qk_lo(a, 1, kT)
                if b:
                    x_lo(5 + a, (2, 3))
                v_lo(a)
                a, t = 2 * b + 1, None if b else 7
                qk_lo(a, 1, kT)
                x_lo(5 + a)
                maximum(b, 0)
                maximum(b, 1)
                if t:
                    ln_stats(t, range(RT), XN_LOADS[t])
                p_lo(b, 0)
                qk_lo(a, 0, qT)
                p_lo(b, 1)
                v_lo(a)
                for g in range(QT // 2):
                    if g:
                        p_lo(b, 2 * g)
                    if g < 3:
                        maximum(b, 2 * g + 2)
                    if g:
                        p_lo(b, 2 * g + 1)
                    inverse(b, 2 * g)
                    inverse(b, 2 * g + 1)
                    if g < 3:
                        maximum(b, 2 * g + 3)
                    if t and g == 1:
                        ln_var(t)
                    if t and g == 3:
                        ln_apply(t, range(RT))
                    if b and g == 3:
                        unpack(1, 0)
                        dequantise(1, 0)
                    dve.wait_ge(s_ohi, 4 * b + g + 1)
                    dve.tensor_tensor(out=oT[:, g % 2, 1, :], in0=ps[:, PV_BANK, 0:2 * P], in1=f32(oT[:, g % 2, 0, :]),
                                      op=ALU.subtract).then_inc(s_olo, 1)
                if b:
                    dequantise(1, 1)
                else:
                    x_lo(7, (0, 1))

            ffn_round(1, 0, True, True)
            with dve.Fori(1, ROUNDS - 1) as c:
                ffn_round(1, c, False, True)
            ffn_round(1, ROUNDS - 1, False, False)

        @block.gpsimd
        def _(pool):
            def deviation(t):
                pool.wait_ge(s_var, 2 * (t + 1))
                pool.tensor_tensor(out=rstd[:, :], in0=rstd[:, :], in1=mhalf[:, :], op=ALU.pow).then_inc(s_rstd, 1)

            def w_lo(phase, u):
                if u >= UNITS:
                    return
                item = ITEM_FFN[phase] + u
                pool.wait_ge(s_whi, item + 1)
                pool.tensor_tensor(out=unit_weights(u, 1), in0=unit_view(u, wf[:, item % 2, :]),
                                   in1=f32(unit_weights(u, 0)), op=ALU.subtract).then_inc(s_wlo, 1)

            _, (sc_d, _, _, _, zq_d, _, _) = cuts
            pool.dma_start(sc_d, flat(scales[2], SC_D)).then_inc(d_cut_d, 16)
            pool.dma_start(zq_d, flat(zeros[2], ZC_D)).then_inc(d_cut_d, 16)
            for row, first in ((0, 0), (FOLD, D_FROM)):
                pool.dma_start(idx[row:row + FOLD, DOWN_COLS], spread(g_idx[2][first:first + D_COLS])).then_inc(d_idx_d, 16)
            pool.memset(mhalf[:, :], -0.5).then_inc(s_cst, 1)
            pool.wait_ge(s_cst, 1)
            parts = maker(pool, s_cut)
            pool.wait_ge(d_cut_gu, 64)
            cut_scales(pool, parts, *cuts[0])
            pool.wait_ge(d_cut_d, 32)
            cut_scales(pool, parts, *cuts[1])
            deviation(0)
            pool.wait_ge(d_grp, 16)
            pool.wait_ge(d_idx_d, 32)
            clamp_and_compare(pool, maker(pool, s_ohd), DOWN_COLS, GD, 1, oh_d[:, :])

            def ffn(phase):
                for u in range(phase, UNITS):
                    if u == 16:
                        deviation(8 * phase + 1)
                    w_lo(phase, u)
                with pool.Fori(1, ROUNDS - 1) as c:
                    deviation(8 * phase + 1 + c)

            ffn(0)
            for k in range(KT):
                pool.wait_ge(s_whi, ITEM_QKV + k + 1)
                pool.tensor_tensor(out=wq[:, 1, k, :], in0=wf[:, (ITEM_QKV + k) % 2, 0:3 * HEAD], in1=f32(wq[:, 0, k, :]),
                                   op=ALU.subtract).then_inc(s_wlo, 1)
            deviation(4)
            deviation(5)
            pool.wait_ge(s_whi, ITEM_O + 1)
            pool.tensor_tensor(out=wo[:, 1, :], in0=wf[:, ITEM_O % 2, :], in1=f32(wo[:, 0, :]), op=ALU.subtract).then_inc(s_wlo, 1)
            pool.wait_ge(d_bo, 16)

            def add_bias(b, tiles):
                for j in tiles:
                    r = j % RT
                    pool.wait_ge(d_res[r], 16 * (5 + 2 * b + j // RT))
                    pool.tensor_tensor(out=xres[:, r, :], in0=xres[:, r, :], in1=bo[:, :], op=ALU.add).then_inc(s_xb, 1)

            def total(b, j):
                pool.wait_ge(s_out, QT * b + j + 1)
                pool.tensor_tensor(out=xres[:, j % RT, :], in0=xres[:, j % RT, :], in1=osb[:, j % 2, :], op=ALU.add)\
                    .then_inc(s_att, 1)

            for b in range(2):
                deviation(6 + 2 * b)
                add_bias(b, range(RT))
                if b == 0:
                    deviation(7)
                for j in range(QT):
                    if not by_dve(b, j):
                        pool.wait_ge(s_xb, QT * b + j + 1)
                        total(b, j)
                    if b and j == RT - 1:
                        w_lo(1, 0)
                    if 2 <= j <= RT + 1:
                        add_bias(b, [j - 2 + RT])
            ffn(1)


def kernel(**inputs):
    import concourse.bacc as bacc
    from concourse.bass_utils import run_bass_kernel_spmd

    nc = bacc.Bacc("TRN2", target_bir_lowering=False, num_devices=1)
    arrays = {}

    def take(name, a):
        a = np.ascontiguousarray(a)
        arrays[name] = a
        return nc.dram_tensor(name, a.shape, mybir.dt.from_np(a.dtype), kind="ExternalInput").ap()

    src = {k: take(f"in_{k}", np.asarray(v)) for k, v in inputs.items()}
    ident = take("in_ident", np.eye(P, dtype=np.float32))
    shifts = take("in_shifts", (BITS * (np.arange(P) % PACK)).astype(np.int32)[:, None])
    rows = np.arange(P) % FOLD
    group = np.stack([rows % GK, np.where(rows < Z_ROW, rows % GD, rows - Z_ROW)], 1)
    groups = take("in_groups", np.concatenate([group, group - [GK, GD]], 1).astype(np.float32))
    out = nc.dram_tensor("out_0", (TOKENS, HID), F32, kind="ExternalOutput").ap()
    mats = ("gate", "up", "down")
    macaron(nc, src["L0_attn_x"].rearrange("b s c -> (b s) c"), src["L0_attn_Wqkv"], src["L0_attn_bqkv"],
            src["L0_attn_Wo"], src["L0_attn_bo"], [src[f"L0_ffn_{m}_qweight"] for m in mats],
            [src[f"L0_ffn_{m}_scales"] for m in mats], [src[f"L0_ffn_{m}_qzeros"] for m in mats],
            [src[f"L0_ffn_{m}_g_idx"] for m in mats], ident, shifts, groups, out)
    r = run_bass_kernel_spmd(nc, [arrays], core_ids=[0])
    return r.results[0]["out_0"].reshape(inputs["L0_attn_x"].shape)
```

```python
from contextlib import ExitStack

import numpy as np

import concourse.bass as bass
from concourse import mybir

F32 = mybir.dt.float32
F32R = mybir.dt.float32r
BF16 = mybir.dt.bfloat16
I32 = mybir.dt.int32
ALU = mybir.AluOpType
ACT = mybir.ActivationFunctionType
AX_X = mybir.AxisListType.X

P = 128
TOKENS, HID, INTER = 2048, 512, 1376
PACK, BITS, GROUP = 8, 4, 128
ROWS = 512
ROUNDS = TOKENS // ROWS
RT = ROWS // P
KT = HID // P
NT = -(-INTER // P)
GK, GD = HID // GROUP, INTER // GROUP
HEAD = HID // 4
SEQ = 1024
QT = SEQ // P
EPS = 1e-5
SCALE = float(np.float32(1.0) / np.sqrt(np.float32(HEAD)))
DEQUANT, BACK = "dequant", "back"
PASSES = ((0, 0), (0, 1), (1, 0))

UNITS = 3 * NT
QSLOTS = 6
KEPT = 2
SAVED = 3 * KEPT
WSLOTS = 6
AHEAD = 4
ITEM_QKV = UNITS
ITEM_O = UNITS + KT
ITEM_BACK = UNITS + KT + 1
Z_ROW = 32
FOLD = 64
D_TILES = 6
D_COLS = D_TILES * P
D_FROM = INTER - D_COLS


def width(i):
    return min(P, INTER - i * P)


def macaron(nc, x, w_qkv, b_qkv, w_o, b_o, packed, scales, zeros, g_idx, ident, shifts, groups, out):
    ctx = ExitStack()
    with ctx:
        at = [-(-nc.sbuf_base // 64) * 64]

        def place(name, shape, dtype, offset=None):
            size = int(np.prod(shape[1:])) * (2 if dtype == BF16 else 4)
            t = nc.alloc_sbuf_tensor_at(name, shape, dtype, offset=at[0] if offset is None else offset)
            if offset is None:
                at[0] += -(-size // 32) * 32
            return t

        w_at = at[0]
        TILE_BYTES = 2 * 3 * HID * 4
        weights = place("weights", [P, NT, 2, 3, HID], F32R)
        xT = place("xT", [P, 2, KT, ROWS], F32R)
        xn = place("xn", [P, RT, HID], F32)
        xres = place("xres", [P, RT, HID], F32)
        hs = place("hs", [P, 2, ROWS], F32)
        hT = place("hT", [P, 2, 2, ROWS], F32R)
        qs_at = at[0]
        qs = place("qs", [P, QSLOTS, KT, P], I32)
        wf = place("wf", [P, 2, KT * P], F32)
        wi = place("wi", [P, KT * P], BF16)
        tab_gu = place("tab_gu", [P, INTER], BF16)
        tab_d = place("tab_d", [P, HID], BF16)
        oh_gu = place("oh_gu", [P, HID], BF16)
        oh_d = place("oh_d", [P, D_COLS], BF16)
        idt = place("idt", [P, P], F32)
        shift = place("shift", [P, 1], I32)
        grp = place("grp", [P, 4], F32)
        bqkv = place("bqkv", [P, 3], F32)
        stats = place("stats", [P, RT, 6], F32)
        mv = place("mv", [P, RT, 2], F32)
        rstd = place("rstd", [P, RT], F32)
        mhalf = place("mhalf", [P, RT], F32)
        spare = place("spare", [P, 1], F32)
        assert at[0] <= nc.sbuf_usable_end, at[0]

        tmp_at = w_at + 9 * TILE_BYTES
        idx = place("idx", [P, HID + D_COLS], I32, tmp_at)
        idf = place("idf", [P, HID + D_COLS], F32, tmp_at + (HID + D_COLS) * 4)
        free = [w_at + 7 * TILE_BYTES]

        def scratch(name, shape, dtype):
            t = place(name, shape, dtype, free[0])
            free[0] += -(-int(np.prod(shape[1:])) * (2 if dtype == BF16 else 4) // 32) * 32
            return t

        SC = GK * INTER // P
        ZP = 16
        ZC = GK * INTER // PACK // ZP
        SP_D, SC_D = 8 * GD, HID // 8
        ZP_D, ZC_D = 4 * GD, HID // PACK // 4
        cuts = []
        for kind, n_p, n_c, z_p, z_c in (("gu", P, 2 * SC, 2 * ZP, ZC), ("d", SP_D, SC_D, ZP_D, ZC_D)):
            cuts.append((
                scratch(f"sc_{kind}", [P, n_c], F32)[0:n_p, :],
                scratch(f"rest_{kind}", [P, n_c], F32)[0:n_p, :],
                scratch(f"rest2_{kind}", [P, n_c], F32)[0:n_p, :],
                scratch(f"parts_{kind}", [P, 3, n_c], BF16)[0:n_p, :, :],
                scratch(f"zq_{kind}", [P, z_c], I32)[0:z_p, :],
                scratch(f"zi_{kind}", [P, z_c, PACK], I32)[0:z_p, :, :],
                scratch(f"zb_{kind}", [P, z_c, PACK], BF16)[0:z_p, :, :]))
        assert free[0] <= tmp_at

        wq = place("wq", [P, 2, KT, 3 * HEAD], F32R, qs_at)
        wback = place("wback", [P, WSLOTS, KT * P], F32, qs_at)
        over = [w_at + KEPT * TILE_BYTES]

        def place_over(name, shape, dtype):
            t = place(name, shape, dtype, over[0])
            over[0] += int(np.prod(shape[1:])) * 4
            return t

        xn_odd = place_over("xn_odd", [P, RT, HID], F32)
        wo = place_over("wo", [P, 2, HID], F32R)
        bo = place_over("bo", [P, HID], F32)
        qT = place_over("qT", [P, 2, SEQ], F32R)
        kT = place_over("kT", [P, 2, SEQ], F32R)
        vt = place_over("vt", [P, ROWS], F32)
        v = place_over("v", [P, 2, QT, HEAD], F32R)
        pr = place_over("pr", [P, 2, SEQ], F32)
        pT = place_over("pT", [P, 2, 2, QT, 2 * P], F32R)
        oT = place_over("oT", [P, 2, 2, 2 * P], F32R)
        xT_odd = place_over("xT_odd", [P, 2, KT, ROWS], F32R)
        osb = place_over("osb", [P, 2, HID], F32)
        mx = place_over("mx", [P, QT], F32)
        nmx = place_over("nmx", [P, QT], F32)
        sums = place_over("sums", [P, QT], F32)
        rinv = place_over("rinv", [P, QT], F32)
        assert over[0] <= w_at + NT * TILE_BYTES

        def x_rows(t):
            return xn_odd if isinstance(t, int) and t in (5, 7) else xn

        def x_turned(t):
            return xT_odd if isinstance(t, int) and t in (5, 7) else xT

        XN_LOADS = {6: 5, 7: 2, 8: 6}

        ps = ctx.enter_context(nc.psum_tensor("ps", [P, 8, 512], F32))
        TURN_BANK = (2, 3, 0, 1)
        Z_BANK, S_BANK, DOWN_BANK = 2, 3, 4

        def pair_of(first, i):
            return 2 if first and i == 0 else 0 if first == DEQUANT else i % 2

        def turn_bank(t, k):
            return 4 + k if isinstance(t, int) and t == 0 else TURN_BANK[k]

        PT_BANK, PV_BANK, OUT_BANK = 2, 0, 1
        Q_BANK, K_BANK, V_BANK, VT_BANK = (5, 1), (6, 4), (4, 0), (7, 0)
        QKV_ORDER = ((2, 0, 1), (1, 2, 0))

        saved = nc.dram_tensor("saved", [UNITS - SAVED, P, KT * P], F32, kind="Internal").ap()
        stream = nc.dram_tensor("stream", [2 * TOKENS, HID], F32, kind="Internal").ap()

        def sem(name):
            return ctx.enter_context(nc.semaphore(name))

        d_small, d_grp, d_cut_gu, d_cut_d, d_idx_gu, d_idx_d, d_xn, d_xn_odd, d_bqkv, d_wo, d_bo = (
            sem(n) for n in ("d_small", "d_grp", "d_cut_gu", "d_cut_d", "d_idx_gu", "d_idx_d", "d_xn", "d_xn_odd", "d_bqkv", "d_wo", "d_bo"))
        d_q = [sem(f"d_q{n}") for n in range(QSLOTS)]
        d_tab = [sem(f"d_tab{n}") for n in range(4)]
        d_wf = [sem(f"d_wf{n}") for n in range(2)]
        d_save = [sem(f"d_save{n}") for n in range(2)]
        d_back = [sem(f"d_back{n}") for n in range(WSLOTS)]
        d_x0 = [sem(f"d_x0{n}") for n in range(RT)]
        d_res = [sem(f"d_res{n}") for n in range(RT)]
        d_st = [sem(f"d_st{n}") for n in range(RT)]
        s_gate, s_up, s_down, s_rows, s_turn, s_sz = (
            sem(n) for n in ("s_gate", "s_up", "s_down", "s_rows", "s_turn", "s_sz"))
        s_qkv, s_vturn, s_score, s_pturn, s_pv, s_proj = (
            sem(n) for n in ("s_qkv", "s_vturn", "s_score", "s_pturn", "s_pv", "s_proj"))
        s_silu, s_hhi, s_xhi, s_whi, s_qkvhi, s_exp, s_phi, s_ohi, s_out = (
            sem(n) for n in ("s_silu", "s_hhi", "s_xhi", "s_whi", "s_qkvhi", "s_exp", "s_phi", "s_ohi", "s_out"))
        s_h, s_hlo, s_xlo, s_sum, s_bn, s_var, s_ln, s_int, s_unp, s_wf, s_tab, s_oh = (
            sem(n) for n in ("s_h", "s_hlo", "s_xlo", "s_sum", "s_bn", "s_var", "s_ln", "s_int", "s_unp", "s_wf", "s_tab", "s_oh"))
        s_qkvlo, s_max, s_nmx, s_plo, s_olo, s_rinv, s_last = (
            sem(n) for n in ("s_qkvlo", "s_max", "s_nmx", "s_plo", "s_olo", "s_rinv", "s_last"))
        s_cst, s_cut, s_ohd, s_rstd, s_wlo, s_xb, s_att = (
            sem(n) for n in ("s_cst", "s_cut", "s_ohd", "s_rstd", "s_wlo", "s_xb", "s_att"))

        def by_dve(b, j):
            return b == 1 and j >= QT - 2

        def out_bank(b, j):
            return DOWN_BANK + 2 + j % 2 if by_dve(b, j) else OUT_BANK

        def f32(ap):
            return ap.bitcast(F32)

        def unit(u):
            return u % 3, u // 3

        def unit_view(u, flat):
            m, i = unit(u)
            if m == 2:
                return flat[0:width(i), :]
            return flat.rearrange("p (k c) -> p k c", k=KT)[:, :, 0:width(i)]

        def unit_weights(u, half):
            m, i = unit(u)
            return unit_view(u, weights[:, i, half, m, :])

        q_count = [0] * QSLOTS
        q_ready = {}
        for n in range(UNITS):
            q_count[n % QSLOTS] += 16 * (1 if n % 3 == 2 else KT)
            q_ready[n] = q_count[n % QSLOTS]

        def saves_before(u):
            return 16 * len(range(SAVED + (SAVED + u) % 2, u, 2))

        SAVES = [saves_before(UNITS + (UNITS + n) % 2) for n in range(2)]

        def row_tiles(dram, first):
            return dram[bass.ds(first, ROWS), :].rearrange("(r p) c -> p r c", p=P)

        def flat(ap, n_cols):
            return ap.rearrange("g n -> (g n)").rearrange("(p c) -> p c", c=n_cols)

        def spread(indices):
            return indices.rearrange("(o n) -> o n", o=1).to_broadcast([FOLD, indices.shape[0]])

        def table(eng, m, at_row=0):
            if m == 2:
                (_, _, _, parts, _, _, zb), dst, g, done = cuts[1], tab_d, GD, d_tab[3 if at_row else 2]
            else:
                (_, _, _, parts, _, _, zb), dst, g, done, at_row = cuts[0], tab_gu, GK, d_tab[m], FOLD * m
                parts, zb = parts[:, :, m * SC:(m + 1) * SC], zb[m * ZP:(m + 1) * ZP, :, :]
            for j in range(3):
                eng.dma_start(dst[at_row + j * g:at_row + (j + 1) * g, :], parts[:, j, :]).then_inc(done, 16)
            row = at_row + Z_ROW
            eng.dma_start(dst[row:row + g, :], zb.rearrange("p c j -> p (c j)")).then_inc(done, 16)

        def maker(eng, semaphore):
            made = [0]

            def step(*instructions):
                for make in instructions:
                    make().then_inc(semaphore, 1)
                    made[0] += 1
                eng.wait_ge(semaphore, made[0])
            return step

        CUT_STEPS, ZERO_STEPS = 5, PACK + 1

        def cut_scales(eng, step, sc, rest, rest2, parts, zq, zi, zb):
            step(lambda: eng.tensor_copy(parts[:, 0, :], sc))
            step(lambda: eng.tensor_tensor(out=rest, in0=sc, in1=parts[:, 0, :], op=ALU.subtract))
            step(lambda: eng.tensor_copy(parts[:, 1, :], rest))
            step(lambda: eng.tensor_tensor(out=rest2, in0=rest, in1=parts[:, 1, :], op=ALU.subtract))
            step(lambda: eng.tensor_copy(parts[:, 2, :], rest2))

        def unpack_zeros(eng, step, sc, rest, rest2, parts, zq, zi, zb):
            step(*(lambda j=j: eng.tensor_scalar(zi[:, :, j], zq, BITS * j, 15, ALU.logical_shift_right, ALU.bitwise_and)
                   for j in range(PACK)))
            step(lambda: eng.tensor_scalar(zb.rearrange("p c j -> p (c j)"), zi.rearrange("p c j -> p (c j)"),
                                           1.0, None, ALU.add))

        def clamp_and_compare(eng, step, cols, n_groups, which, dst):
            step(lambda: eng.tensor_scalar(idf[:, cols], idx[:, cols], -float(n_groups), n_groups - 1.0, ALU.max, ALU.min))
            step(lambda: eng.tensor_scalar(dst, idf[:, cols], grp[:, which + 2:which + 3], None, ALU.is_equal))

        def one_hot(eng, step, cols, which, dst):
            step(lambda: eng.scalar_tensor_tensor(out=dst, in0=idf[:, cols], scalar=grp[:, which:which + 1], in1=dst,
                                                  op0=ALU.is_equal, op1=ALU.add))

        GU_COLS, DOWN_COLS = slice(0, HID), slice(HID, HID + D_COLS)

        block = ctx.enter_context(nc.Block())

        @block.sync
        def _(sp):
            def load_round(dram, first, t):
                odd = x_rows(t) is xn_odd
                sp.wait_ge(s_turn, KT * (t - (1 if odd or t in (6, 8) else 0)) if isinstance(t, int) else KT * t)
                sp.dma_start(x_rows(t)[:, :, :], row_tiles(dram, first)).then_inc(d_xn_odd if odd else d_xn, 16)

            def load_residual(dram, first, t, slots=range(RT)):
                for r in slots:
                    row = first + r * P
                    sp.wait_ge(d_st[r], 16 * t)
                    sp.dma_start(xres[:, r, :], dram[bass.ds(row, P), :]).then_inc(d_res[r], 16)

            def load_units(units):
                for u in units:
                    m, i = unit(u)
                    s = u % QSLOTS
                    if u >= QSLOTS:
                        sp.wait_ge(s_int, u - QSLOTS + 1)
                    kt = range(1) if m == 2 else range(KT)
                    for k in kt:
                        if m == 2:
                            rows = packed[2][i * 16:i * 16 + width(i) // PACK, :]
                            dst = unit_view(u, qs[:, s, :, :].rearrange("p k c -> p (k c)"))
                        else:
                            rows = packed[m][k * 16:(k + 1) * 16, i * P:i * P + width(i)]
                            dst = qs[:, s, k, 0:width(i)]
                        n_rows, n_cols = rows.shape
                        src = rows.rearrange("r (o c) -> r o c", o=1).to_broadcast([n_rows, PACK, n_cols])
                        sp.dma_start(dst, src).then_inc(d_q[s], 16)

            def save(u):
                sp.wait_ge(s_wf, u + 1)
                sp.dma_start(unit_view(u, saved[u - SAVED]), unit_view(u, wf[:, u % 2, :])).then_inc(d_save[u % 2], 16)

            def bring_back(u):
                n = u - SAVED
                if n >= WSLOTS:
                    sp.wait_ge(s_wlo, ITEM_BACK + n - WSLOTS + 1)
                sp.dma_start(unit_view(u, wback[:, n % WSLOTS, :]), unit_view(u, saved[n])).then_inc(d_back[n % WSLOTS], 16)

            def store_round(dram, first, f):
                for r in range(RT):
                    row = first + r * P
                    count = RT * f + r + 1
                    if not isinstance(count, int):
                        count = sp.to_reg(count)
                        sp.wait_ge(s_tab, 5)
                    sp.wait_ge(s_sum, count)
                    sp.dma_start(dram[bass.ds(row, P), :], xres[:, r, :]).then_inc(d_st[r], 16)

            (sc_gu, _, _, _, zq_gu, _, _), _ = cuts
            for m in range(2):
                sp.dma_start(sc_gu[:, m * SC:(m + 1) * SC], flat(scales[m], SC)).then_inc(d_cut_gu, 16)
            for m in range(2):
                sp.dma_start(zq_gu[m * ZP:(m + 1) * ZP, :], flat(zeros[m], ZC)).then_inc(d_cut_gu, 16)
            sp.dma_start(grp[:, :], groups).then_inc(d_grp, 16)
            sp.dma_start(idt[:, :], ident).then_inc(d_small, 16)
            sp.dma_start(shift[:, :], shifts).then_inc(d_small, 16)
            load_units([0])
            sp.wait_ge(s_cut, CUT_STEPS)
            sp.wait_ge(s_tab, ZERO_STEPS)
            table(sp, 1)
            load_units([1, 2])
            sp.wait_ge(s_cut, 2 * CUT_STEPS)
            sp.wait_ge(s_tab, 2 * ZERO_STEPS)
            table(sp, 2)
            load_units([3, 4, 5])
            load_round(x, ROWS, 1)
            load_units(range(QSLOTS, QSLOTS + 2))
            table(sp, 2, FOLD)
            sp.dma_start(bqkv[:, :], b_qkv.rearrange("(j p) -> p j", p=P), allow_slow_non_contiguous=True).then_inc(d_bqkv, 16)

            def ffn(phase):
                src, dst = (x, stream[TOKENS:2 * TOKENS, :])[phase], (stream[0:TOKENS, :], out)[phase]
                t0, f0 = 8 * phase, 4 * phase
                if phase == 0:
                    load_units(range(QSLOTS + 2, SAVED + AHEAD))
                    for u in range(SAVED, UNITS):
                        save(u)
                        if u + AHEAD < UNITS:
                            load_units([u + AHEAD])
                        if u == UNITS // 2:
                            for r in range(RT):
                                sp.dma_start(xres[:, r, :], src[r * P:(r + 1) * P, :]).then_inc(d_res[r], 16)
                else:
                    load_round(src, ROWS, t0 + 1)
                    load_residual(src, 0, t0)
                    for u in range(SAVED + WSLOTS, UNITS):
                        bring_back(u)
                store_round(dst, 0, f0)
                with sp.Fori(0, ROUNDS - 2) as before:
                    c = before + 1
                    load_round(src, ROWS * (c + 1), t0 + c + 1)
                    load_residual(src, ROWS * c, t0 + c)
                    store_round(dst, ROWS * c, f0 + c)
                c = ROUNDS - 1
                if phase == 0:
                    load_round(stream, 0, t0 + ROUNDS)
                load_residual(src, ROWS * c, t0 + c)
                if phase == 0:
                    for n in range(2):
                        sp.wait_ge(d_save[n], SAVES[n])
                    for k in range(KT):
                        item = ITEM_QKV + k
                        sp.wait_ge(s_wlo, item - 1)
                        sp.dma_start(wf[:, item % 2, 0:3 * HEAD], w_qkv[k * P:(k + 1) * P, :]).then_inc(d_wf[item % 2], 16)
                    sp.wait_ge(s_down, NT * c + KEPT + 1)
                    load_round(stream, ROWS, 5)
                    load_round(stream, 2 * ROWS, 6)
                    sp.wait_ge(s_down, NT * c + KEPT + 2)
                    sp.wait_ge(s_wlo, ITEM_O - 1)
                    sp.dma_start(wf[:, ITEM_O % 2, :], w_o).then_inc(d_wo, 16)
                    sp.dma_start(bo[:, :], b_o.rearrange("(o n) -> o n", o=1).to_broadcast([P, HID])).then_inc(d_bo, 16)
                store_round(dst, ROWS * c, f0 + c)

            ffn(0)

            for b in range(2):
                t = 4 + 2 * b
                base = 2 * ROWS * b
                load_residual(stream, base, t)
                if b == 0:
                    load_round(stream, base + 3 * ROWS, t + 3)
                else:
                    sp.wait_ge(s_qkv, 3 * ROUNDS)
                    for u in range(SAVED, SAVED + WSLOTS):
                        bring_back(u)

                def store(j):
                    if by_dve(b, j):
                        sp.wait_ge(s_last, j - QT + 3)
                    else:
                        sp.wait_ge(s_att, QT * b + j + 1)
                    row = TOKENS + base + j * P
                    sp.dma_start(stream[row:row + P, :], xres[:, j % RT, :]).then_inc(d_st[j % RT], 16)

                store(0)
                for j in range(1, RT):
                    store(j)
                    load_residual(stream, base + ROWS, t + 1, [j - 1])
                load_residual(stream, base + ROWS, t + 1, [RT - 1])
                if b == 0:
                    load_round(stream, TOKENS, t + 4)
                for j in range(RT, QT):
                    store(j)

            ffn(1)
            for r in range(RT):
                sp.wait_ge(d_st[r], 16 * 3 * ROUNDS)

        @block.tensor
        def _(pe):
            def product(bank_ap, lhs, rhs, first, last):
                for n, (a, b) in enumerate(PASSES):
                    mm = pe.matmul(bank_ap, lhs(a), rhs(b), start=first and n == 0, stop=last and n == 2)
                return mm

            def keep_warm(n):
                for _ in range(n):
                    pe.matmul(ps[:, 1, 0:P], idt[:, :], idt[:, :], start=True, stop=True)

            def turn(t, kts):
                for k in kts:
                    for r in range(RT):
                        mm = pe.transpose(ps[:, turn_bank(t, k), r * P:(r + 1) * P], x_rows(t)[:, r, k * P:(k + 1) * P],
                                          idt[:, :])
                    mm.then_inc(s_turn, 1)

            def gate_up(i, m, pair, kts=range(KT), by_tile=False):
                w = width(i)
                for k in kts:
                    if by_tile:
                        pe.wait_ge(s_xlo, k + 1)
                    mm = product(ps[0:w, 2 * pair + m, :], lambda h: weights[:, i, h, m, k * P:k * P + w],
                                 lambda h: xT[:, h, k, :],
                                 k == 0, k == KT - 1)
                if k == KT - 1:
                    mm.then_inc((s_gate, s_up)[m], 1)

            def down(i, n):
                w = width(i)
                pe.wait_ge(s_hlo, n + 1)
                for r in range(RT):
                    mm = product(ps[:, DOWN_BANK + r, :], lambda h: hT[0:w, i % 2, h, r * P:(r + 1) * P],
                                 lambda h: weights[0:w, i, h, 2, :], i == 0, i == NT - 1)
                    if i == NT - 1 and r < RT - 1:
                        mm.then_inc(s_rows, 1)
                mm.then_inc(s_down, 1)

            def scales_zeros(u):
                if u >= UNITS:
                    return
                m, i = unit(u)
                w = width(i)
                if u:
                    if u in (2, 3 * D_TILES + 2):
                        if u == 2:
                            pe.wait_ge(s_oh, 4)
                        pe.wait_ge(d_tab[2 if u == 2 else 3], 64)
                    pe.wait_ge(s_wf, u)
                g = (GK, GK, GD)[m]
                row = FOLD if m == 1 or (m == 2 and i >= D_TILES) else 0
                for rows, bank in ((slice(row + Z_ROW, row + Z_ROW + g), Z_BANK), (slice(row, row + 3 * g), S_BANK)):
                    if m == 2:
                        col = i * P - (D_FROM if row else 0)
                        mm = pe.matmul(ps[0:w, bank, :], oh_d[rows, col:col + w], tab_d[rows, :], start=True, stop=True)
                    else:
                        for k in range(KT):
                            mm = pe.matmul(ps[:, bank, k * P:k * P + w], oh_gu[rows, k * P:(k + 1) * P],
                                           tab_gu[rows, i * P:i * P + w], start=True, stop=True)
                mm.then_inc(s_sz, 1)

            def ffn_round(phase, c, first, turn_next):
                f, t = 4 * phase + c, 8 * phase + c
                dequant = first == DEQUANT

                def weights_of(i, m):
                    if dequant:
                        pe.wait_ge(s_wlo, 3 * i + m + 1)
                    elif first == BACK and i >= KEPT:
                        pe.wait_ge(s_wlo, ITEM_BACK + 3 * i + m - SAVED + 1)

                if first is None:
                    pe.wait_ge(s_xlo, KT * (t + 1))
                for i in range(NT):
                    n = NT * f + i
                    pair = pair_of(first, i)
                    if first == BACK and i == 0:
                        continue
                    weights_of(i, 0)
                    if i >= 2:
                        pe.wait_ge(s_h, n if dequant else n - 1)
                    if dequant and i == 0:
                        gate_up(0, 0, pair, by_tile=True)
                        scales_zeros(2)
                        weights_of(0, 1)
                        gate_up(0, 1, pair, (0, 1))
                        scales_zeros(3)
                        gate_up(0, 1, pair, (2, 3))
                        scales_zeros(4)
                        keep_warm(6)
                        continue
                    if dequant and i == 1:
                        gate_up(i, 0, pair, (0, 1))
                        scales_zeros(5)
                        gate_up(i, 0, pair, (2, 3))
                    else:
                        gate_up(i, 0, pair)
                    if dequant:
                        scales_zeros(3 * i + 3)
                    weights_of(i, 1)
                    gate_up(i, 1, pair)
                    if dequant:
                        scales_zeros(3 * i + 4)
                    if i == 0:
                        continue
                    if i == NT - 1:
                        break
                    if i == 1:
                        if first is None:
                            pe.wait_ge(s_sum, RT * f)
                        elif first == BACK:
                            pe.wait_ge(s_last, 2)
                    weights_of(i - 1, 2)
                    down(i - 1, n - 1)
                    if dequant:
                        scales_zeros(3 * i + 5)
                n = NT * f + NT - 1
                if turn_next:
                    pe.wait_ge(s_ln, RT * (t + 2))
                    if dequant:
                        pe.wait_ge(s_wf, UNITS)
                    else:
                        pe.wait_ge(s_h, n)
                    turn(t + 1, (0, 1))
                weights_of(NT - 1, 2)
                down(NT - 2, n - 1)
                if turn_next:
                    pe.wait_ge(s_h, n + 1)
                    turn(t + 1, (2, 3))
                down(NT - 1, n)

            def qkv_product(a, j):
                half = a % 2
                src = x_turned(4 + a)
                for k in range(KT):
                    if j == QKV_ORDER[half][0]:
                        pe.wait_ge(s_xlo, KT * (4 + a) + k + 1)
                    mm = product(ps[:, (Q_BANK, K_BANK, V_BANK)[j][half], :], lambda h: wq[:, h, k, j * HEAD:(j + 1) * HEAD],
                                 lambda h: src[:, h, k, :], k == 0, k == KT - 1)
                mm.then_inc(s_qkv, 1)

            def turn_v(a):
                pe.wait_ge(s_qkvhi, 4 * a + (2 if a % 2 else 1))
                for r in range(RT):
                    mm = pe.transpose(ps[:, VT_BANK[a % 2], r * P:(r + 1) * P], vt[:, r * P:(r + 1) * P], idt[:, :])
                mm.then_inc(s_vturn, 1)

            def qkv_first(a):
                t = 4 + a
                if a == 0:
                    pe.wait_ge(s_ln, RT * (t + 2))
                    pe.wait_ge(s_xlo, KT * (t + 1))
                    turn(t + 1, range(KT))
                    pe.wait_ge(s_sum, RT * ROUNDS - 3)
                    pe.wait_ge(s_wlo, ITEM_O)
                    qkv_product(a, 2)
                    pe.wait_ge(s_sum, RT * ROUNDS)
                    qkv_product(a, 0)
                qkv_product(a, 1)
                if a:
                    pe.wait_ge(s_out, QT)
                    turn(t + 1, (2, 3))
                turn_v(a)

            def qkv_second(a):
                t, b = 4 + a, a // 2
                pe.wait_ge(s_qkvhi, 4 * (a - 1) + 1)
                qkv_product(a, 1)
                pe.wait_ge(s_ln, RT * (t + 2))
                turn(t + 1, range(KT))
                pe.wait_ge(s_qkvlo, 3 * a + 1)
                score(b, 0)
                score(b, 1)
                pe.wait_ge(s_xlo, KT * (t + 1) + 3)
                qkv_product(a, 2)
                turn_p(b, 0)
                pe.wait_ge(s_xlo, KT * (t + 1) + 4)
                qkv_product(a, 0)
                turn_p(b, 1)
                turn_v(a)

            def score(b, j):
                m = QT * b + j
                if j >= 2:
                    pe.wait_ge(s_exp, m - 1)
                for half in range(2):
                    mm = product(ps[:, 4 + 2 * (j % 2) + half, :], lambda h: qT[:, h, j * P:(j + 1) * P],
                                 lambda h: kT[:, h, half * 512:(half + 1) * 512], True, True)
                mm.then_inc(s_score, 1)

            def turn_p(b, j):
                m = QT * b + j
                pe.wait_ge(s_exp, m + 1)
                for half in range(2):
                    if j:
                        pe.wait_ge(s_plo, 2 * m + half - 1)
                    for k in range(4):
                        c = half * 4 + k
                        mm = pe.transpose(ps[:, PT_BANK + half, k * P:(k + 1) * P], pr[:, j % 2, c * P:(c + 1) * P], idt[:, :])
                    mm.then_inc(s_pturn, 1)

            def pv(b, g):
                pe.wait_ge(s_plo, 2 * QT * b + 4 * g + 4)
                if g:
                    pe.wait_ge(s_olo, 4 * b + g)
                for c in range(QT):
                    mm = product(ps[:, PV_BANK, 0:2 * P], lambda h: v[:, h, c, :], lambda h: pT[:, g % 2, h, c, :],
                                 c == 0, c == QT - 1)
                mm.then_inc(s_pv, 1)

            def project(b, j):
                g = j // 2
                pe.wait_ge(s_olo, 4 * b + g + 1)
                if j and not by_dve(b, j):
                    pe.wait_ge(s_out, QT * b + j)
                product(ps[:, out_bank(b, j), :], lambda h: oT[:, g % 2, h, (j % 2) * P:(j % 2 + 1) * P],
                        lambda h: wo[:, h, :], True, True).then_inc(s_proj, 1)

            pe.wait_ge(d_small, 32)
            keep_warm(10)
            for r in range(RT):
                pe.wait_ge(s_ln, r + 1)
                for k in range(KT):
                    mm = pe.transpose(ps[:, turn_bank(0, k), r * P:(r + 1) * P], xn[:, r, k * P:(k + 1) * P], idt[:, :])
                    if r == RT - 1:
                        mm.then_inc(s_turn, 1)
            pe.wait_ge(d_tab[0], 64)
            pe.wait_ge(s_oh, 3)
            scales_zeros(0)
            keep_warm(6)
            pe.wait_ge(d_tab[1], 64)
            scales_zeros(1)
            keep_warm(6)
            ffn_round(0, 0, DEQUANT, True)
            with pe.Fori(1, ROUNDS) as c:
                ffn_round(0, c, None, True)

            for b in range(2):
                qkv_first(2 * b)
                qkv_second(2 * b + 1)
                for g in range(QT // 2):
                    for j in (2 * g, 2 * g + 1):
                        if g:
                            turn_p(b, j)
                            if j == 2:
                                pe.wait_ge(s_wlo, ITEM_O + 1)
                            project(b, j - 2)
                        if g < 3:
                            score(b, j + 2)
                    if g == 0:
                        pe.wait_ge(s_qkvlo, 3 * (2 * b + 2))
                    if g == 3:
                        if b == 0:
                            qkv_product(2, 2)
                        else:
                            gate_up(0, 0, pair_of(BACK, 0))
                    pv(b, g)
                if b:
                    gate_up(0, 1, pair_of(BACK, 0))
                else:
                    pe.wait_ge(s_ln, RT * 8)
                    turn(7, (0, 1))
                project(b, QT - 2)
                if b == 0:
                    qkv_product(2, 0)
                project(b, QT - 1)
            pe.wait_ge(s_out, 2 * QT - 2)

            ffn_round(1, 0, BACK, True)
            with pe.Fori(1, ROUNDS - 1) as c:
                ffn_round(1, c, None, True)
            ffn_round(1, ROUNDS - 1, None, False)

        @block.scalar
        def _(act):
            def x_hi(t, kts=range(KT)):
                for k in kts:
                    act.wait_ge(s_turn, KT * t + k + 1)
                    act.activation(x_turned(t)[:, 0, k, :], ps[:, turn_bank(t, k), :], ACT.Copy).then_inc(s_xhi, 1)

            def w_hi(u):
                if u >= UNITS:
                    return
                act.wait_ge(s_wf, u + 1)
                act.activation(unit_weights(u, 0), unit_view(u, wf[:, u % 2, :]), ACT.Copy).then_inc(s_whi, 1)

            def back_hi(u):
                if u >= UNITS:
                    return
                n = u - SAVED
                act.wait_ge(d_back[n % WSLOTS], 16 * (n // WSLOTS + 1))
                act.activation(unit_weights(u, 0), unit_view(u, wback[:, n % WSLOTS, :]), ACT.Copy).then_inc(s_whi, 1)

            def ffn_round(phase, c, first, turn_next, last_of_first=False):
                f, t = 4 * phase + c, 8 * phase + c
                dequant = first == DEQUANT
                if dequant:
                    w_hi(1)
                for i in range(NT):
                    n = NT * f + i
                    w = width(i)
                    pair = pair_of(first, i)
                    act.wait_ge(s_gate, n + 1)
                    if not dequant or i >= 2:
                        act.wait_ge(s_hlo, n - 1)
                    act.activation(hs[0:w, i % 2, :], ps[0:w, 2 * pair, :], ACT.Silu).then_inc(s_silu, 1)
                    if dequant:
                        for u in (2, 3) if i == 0 else (3 * i + 3,):
                            w_hi(u)
                    act.wait_ge(s_h, n + 1)
                    if not dequant or i >= 2:
                        act.wait_ge(s_down, n - 1)
                    act.activation(hT[0:w, i % 2, 0, :], hs[0:w, i % 2, :], ACT.Copy).then_inc(s_hhi, 1)
                    if dequant:
                        w_hi(3 * i + 4)
                        w_hi(3 * i + 5)
                    if first == BACK:
                        if i == 0:
                            act.wait_ge(s_last, 2)
                        for m in range(3):
                            back_hi(3 * (i + KEPT) + m)
                    if last_of_first and 1 <= i <= KT:
                        slot = (ITEM_QKV + i - 1) % 2
                        act.wait_ge(d_wf[slot], 16 * ((i + 1) // 2))
                        act.activation(wq[:, 0, i - 1, :], wf[:, slot, 0:3 * HEAD], ACT.Copy).then_inc(s_whi, 1)
                if turn_next:
                    x_hi(t + 1)

            for r in range(RT):
                act.dma_start(xn[:, r, :], x[r * P:(r + 1) * P, :]).then_inc(d_x0[r], 16)
            for m in range(2):
                act.dma_start(idx[FOLD * m:FOLD * m + FOLD, GU_COLS], spread(g_idx[m])).then_inc(d_idx_gu, 16)
            act.wait_ge(s_cut, CUT_STEPS)
            act.wait_ge(s_tab, ZERO_STEPS)
            table(act, 0)
            x_hi(0)
            w_hi(0)
            ffn_round(0, 0, DEQUANT, True)
            with act.Fori(1, ROUNDS - 1) as c:
                ffn_round(0, c, None, True)
            ffn_round(0, ROUNDS - 1, None, True, last_of_first=True)
            act.wait_ge(d_bqkv, 16)
            act.wait_ge(d_wo, 16)
            act.activation(wo[:, 0, :], wf[:, ITEM_O % 2, :], ACT.Copy).then_inc(s_whi, 1)

            def p_hi(b, j):
                m, g = QT * b + j, j // 2
                for half in range(2):
                    act.wait_ge(s_pturn, 2 * m + half + 1)
                    if g >= 2 and j % 2 == 0 and half == 0:
                        act.wait_ge(s_pv, 4 * b + g - 1)
                    act.activation(pT[:, g % 2, 0, 4 * half:4 * half + 4, (j % 2) * P:(j % 2 + 1) * P],
                                   ps[:, PT_BANK + half, :].rearrange("p (k c) -> p k c", k=4), ACT.Copy).then_inc(s_phi, 1)

            def exp(b, j):
                m = QT * b + j
                act.wait_ge(s_nmx, m + 1)
                if j >= 2:
                    act.wait_ge(s_pturn, 2 * m - 2)
                act.activation(pr[:, j % 2, :], ps[:, 4 + 2 * (j % 2):6 + 2 * (j % 2), :].rearrange("p a c -> p (a c)"), ACT.Exp,
                               bias=nmx[:, j:j + 1], scale=SCALE, accum_out=sums[:, j:j + 1]).then_inc(s_exp, 1)

            def scaled(b, j):
                m = QT * b + j
                act.wait_ge(s_rinv, m + 1)
                act.wait_ge(s_proj, m + 1)
                if m >= 2:
                    act.wait_ge(s_att, m - 1)
                act.activation(osb[:, j % 2, :], ps[:, OUT_BANK, :], ACT.Copy, scale=rinv[:, j:j + 1]).then_inc(s_out, 1)

            def v_bias(a):
                act.wait_ge(s_qkv, 3 * a + (2 if a % 2 else 1))
                act.activation(vt[:, :], ps[:, V_BANK[a % 2], :], ACT.Identity, bias=bqkv[:, 2:3]).then_inc(s_qkvhi, 1)

            def qk_hi(a, j, dst):
                half = a % 2
                act.wait_ge(s_qkv, 3 * a + QKV_ORDER[half].index(j) + 1)
                act.activation(dst[:, 0, half * ROWS:(half + 1) * ROWS], ps[:, (Q_BANK, K_BANK)[j][half], :], ACT.Identity,
                               bias=bqkv[:, j:j + 1]).then_inc(s_qkvhi, 1)

            def v_hi(a):
                half = a % 2
                act.wait_ge(s_vturn, a + 1)
                act.activation(v[:, 0, 4 * half:4 * half + 4, :].rearrange("p c d -> p (c d)"), ps[:, VT_BANK[half], :], ACT.Copy)\
                    .then_inc(s_qkvhi, 1)

            for b in range(2):
                a = 2 * b
                if b == 0:
                    x_hi(5)
                    v_bias(0)
                qk_hi(a, 0, qT)
                qk_hi(a, 1, kT)
                if b:
                    x_hi(5 + a, (2, 3))
                v_hi(a)
                a = 2 * b + 1
                qk_hi(a, 1, kT)
                x_hi(5 + a)
                exp(b, 0)
                exp(b, 1)
                v_bias(a)
                p_hi(b, 0)
                qk_hi(a, 0, qT)
                p_hi(b, 1)
                v_hi(a)
                for g in range(QT // 2):
                    for j in (2 * g, 2 * g + 1):
                        if g:
                            p_hi(b, j)
                            scaled(b, j - 2)
                    if g < 3:
                        exp(b, 2 * g + 2)
                    if g in (1, 2):
                        exp(b, 2 * g + 3)
                    if b == 0 and g == 3:
                        v_bias(2)
                    act.wait_ge(s_pv, 4 * b + g + 1)
                    if g >= 2:
                        act.wait_ge(s_proj, QT * b + 2 * g - 2)
                    act.activation(oT[:, g % 2, 0, :], ps[:, PV_BANK, 0:2 * P], ACT.Copy).then_inc(s_ohi, 1)
                    if g == 0:
                        exp(b, 3)
                if b == 0:
                    x_hi(7, (0, 1))
                    scaled(b, QT - 2)
                    scaled(b, QT - 1)

            ffn_round(1, 0, BACK, True)
            with act.Fori(1, ROUNDS - 1) as c:
                ffn_round(1, c, None, True)
            ffn_round(1, ROUNDS - 1, None, False)

        @block.vector
        def _(dve):
            def ln_stats(t, tiles, n_load=None):
                if n_load is not None:
                    dve.wait_ge(d_xn_odd if x_rows(t) is xn_odd else d_xn, 16 * n_load)
                for r in tiles:
                    if isinstance(t, int) and t == 0:
                        dve.wait_ge(d_x0[r], 16)
                    dve.bn_stats(stats[:, r, :], x_rows(t)[:, r, :]).then_inc(s_bn, 1)

            def ln_var(t):
                dve.wait_ge(s_bn, RT * (t + 1))
                dve.memset(spare[:, :], 0.0)
                for r in range(RT):
                    aggr = dve.bn_aggr(mv[:, r, :], stats[:, r, :])
                aggr.then_inc(s_var, 1)
                dve.wait_ge(s_var, 2 * t + 1)
                dve.tensor_scalar(rstd[:, :], mv[:, :, 1], EPS, None, ALU.add).then_inc(s_var, 1)

            def ln_apply(t, tiles):
                dve.wait_ge(s_rstd, t + 1)
                for r in tiles:
                    dve.tensor_scalar(x_rows(t)[:, r, :], x_rows(t)[:, r, :], mv[:, r, 0:1], rstd[:, r:r + 1],
                                      ALU.subtract, ALU.mult).then_inc(s_ln, 1)

            def x_lo(t, kts=range(KT)):
                dst = x_turned(t)
                for k in kts:
                    dve.wait_ge(s_xhi, KT * t + k + 1)
                    dve.tensor_tensor(out=dst[:, 1, k, :], in0=ps[:, turn_bank(t, k), :], in1=f32(dst[:, 0, k, :]),
                                      op=ALU.subtract).then_inc(s_xlo, 1)

            def unpack(u):
                if u >= UNITS:
                    return
                s = u % QSLOTS
                dve.wait_ge(d_q[s], q_ready[u])
                flat = unit_view(u, qs[:, s, :, :].rearrange("p k c -> p (k c)"))
                dve.tensor_scalar(flat, flat, shift[0:flat.shape[0], 0:1], 15, ALU.logical_shift_right,
                                  ALU.bitwise_and).then_inc(s_unp, 1)

            def dequantise(u, unpack_next=True):
                if u >= UNITS:
                    return
                flat = unit_view(u, qs[:, u % QSLOTS, :, :].rearrange("p k c -> p (k c)"))
                dve.wait_ge(s_unp, u + 1)
                dve.wait_ge(s_sz, u + 1)
                dve.tensor_tensor(out=unit_view(u, wi[:, :]), in0=flat, in1=unit_view(u, ps[:, Z_BANK, :]),
                                  op=ALU.subtract).then_inc(s_int, 1)
                dve.wait_ge(s_int, u + 1)
                if u >= 2:
                    dve.wait_ge(s_wlo, u - 1)
                if u - 2 >= SAVED:
                    dve.wait_ge(d_save[u % 2], saves_before(u))
                dve.tensor_tensor(out=unit_view(u, wf[:, u % 2, :]), in0=unit_view(u, wi[:, :]),
                                  in1=unit_view(u, ps[:, S_BANK, :]), op=ALU.mult).then_inc(s_wf, 1)
                if unpack_next:
                    unpack(u + 1)

            def ffn_round(phase, c, first, turn_next, last_of_first=False):
                f, t = 4 * phase + c, 8 * phase + c
                dequant = first == DEQUANT
                if dequant:
                    dequantise(1)
                    dve.wait_ge(s_ohd, 2)
                    one_hot(dve, compare, DOWN_COLS, 1, oh_d[:, :])
                for i in range(NT):
                    n = NT * f + i
                    w = width(i)
                    pair = pair_of(first, i)
                    if dequant:
                        for u in (2, 3, 4) if i == 0 else (3 * i + 3,):
                            dequantise(u)
                    dve.wait_ge(s_up, n + 1)
                    dve.wait_ge(s_silu, n + 1)
                    dve.tensor_tensor(out=hs[0:w, i % 2, :], in0=hs[0:w, i % 2, :], in1=ps[0:w, 2 * pair + 1, :],
                                      op=ALU.mult).then_inc(s_h, 1)
                    if dequant and i:
                        dequantise(3 * i + 4)
                    if turn_next:
                        if i in (2, 3):
                            ln_stats(t + 1, (2 * i - 4, 2 * i - 3), (c + 1 if phase == 0 else c + 7) if i == 2 else None)
                        if i == 4:
                            ln_var(t + 1)
                        if i in (5, 6):
                            ln_apply(t + 1, (2 * i - 10, 2 * i - 9))
                    if last_of_first:
                        if i in (7, 8):
                            ln_stats(5, (2 * i - 14, 2 * i - 13), 1 if i == 7 else None)
                        if i == 9:
                            ln_var(5)
                        if i == 10:
                            ln_apply(5, range(RT))
                    dve.wait_ge(s_hhi, n + 1)
                    dve.tensor_tensor(out=hT[0:w, i % 2, 1, :], in0=hs[0:w, i % 2, :], in1=f32(hT[0:w, i % 2, 0, :]),
                                      op=ALU.subtract).then_inc(s_hlo, 1)
                    if dequant:
                        dequantise(3 * i + 5)
                if turn_next:
                    x_lo(t + 1)
                for r in range(RT):
                    if r < RT - 1:
                        dve.wait_ge(s_rows, (RT - 1) * f + r + 1)
                    else:
                        dve.wait_ge(s_down, NT * (f + 1))
                    dve.wait_ge(d_res[r], 16 * (t + 1))
                    dve.scalar_tensor_tensor(out=xres[:, r, :], in0=ps[:, DOWN_BANK + r, :], scalar=0.5, in1=xres[:, r, :],
                                             op0=ALU.mult, op1=ALU.add).then_inc(s_sum, 1)

            dve.wait_ge(d_cut_gu, 64)
            tables = maker(dve, s_tab)
            unpack_zeros(dve, tables, *cuts[0])
            ln_stats(0, range(RT))
            ln_var(0)
            dve.wait_ge(d_grp, 16)
            dve.wait_ge(d_idx_gu, 32)
            compare = maker(dve, s_oh)
            clamp_and_compare(dve, compare, GU_COLS, GK, 0, oh_gu[:, :])
            one_hot(dve, compare, GU_COLS, 0, oh_gu[:, :])
            ln_apply(0, range(RT))
            dve.wait_ge(d_small, 32)
            unpack(0)
            dve.wait_ge(d_cut_d, 32)
            unpack_zeros(dve, tables, *cuts[1])
            dequantise(0, unpack_next=False)
            x_lo(0)
            unpack(1)
            ffn_round(0, 0, DEQUANT, True)
            with dve.Fori(1, ROUNDS - 1) as c:
                ffn_round(0, c, None, True)
            ffn_round(0, ROUNDS - 1, None, True, last_of_first=True)

            def maximum(b, j):
                m = QT * b + j
                dve.wait_ge(s_score, m + 1)
                dve.reduce_max(mx[:, j:j + 1], ps[:, 4 + 2 * (j % 2):6 + 2 * (j % 2), :].rearrange("p a c -> p (a c)"), AX_X)\
                    .then_inc(s_max, 1)
                dve.wait_ge(s_max, m + 1)
                dve.tensor_scalar(nmx[:, j:j + 1], mx[:, j:j + 1], -SCALE, None, ALU.mult).then_inc(s_nmx, 1)

            def p_lo(b, j):
                m, g = QT * b + j, j // 2
                for half in range(2):
                    dve.wait_ge(s_phi, 2 * m + half + 1)
                    at_ = (slice(4 * half, 4 * half + 4), slice((j % 2) * P, (j % 2 + 1) * P))
                    dve.tensor_tensor(out=pT[:, g % 2, 1, at_[0], at_[1]],
                                      in0=ps[:, PT_BANK + half, :].rearrange("p (k c) -> p k c", k=4),
                                      in1=f32(pT[:, g % 2, 0, at_[0], at_[1]]), op=ALU.subtract).then_inc(s_plo, 1)

            def inverse(b, j):
                dve.wait_ge(s_exp, QT * b + j + 1)
                dve.reciprocal(rinv[:, j:j + 1], sums[:, j:j + 1]).then_inc(s_rinv, 1)

            def total(b, j):
                m = QT * b + j
                dve.wait_ge(s_rinv, m + 1)
                dve.wait_ge(s_proj, m + 1)
                dve.wait_ge(s_xb, m + 1)
                dve.scalar_tensor_tensor(out=xres[:, j % RT, :], in0=ps[:, out_bank(b, j), :], scalar=rinv[:, j:j + 1],
                                         in1=xres[:, j % RT, :], op0=ALU.mult, op1=ALU.add).then_inc(s_last, 1)

            def qk_lo(a, j, dst):
                half = a % 2
                dve.wait_ge(s_qkvhi, 4 * a + QKV_ORDER[half].index(j) + 1)
                cols = slice(half * ROWS, (half + 1) * ROWS)
                dve.scalar_tensor_tensor(out=dst[:, 1, cols], in0=ps[:, (Q_BANK, K_BANK)[j][half], :], scalar=bqkv[:, j:j + 1],
                                         in1=f32(dst[:, 0, cols]), op0=ALU.add, op1=ALU.subtract).then_inc(s_qkvlo, 1)

            def v_lo(a):
                half = a % 2
                dve.wait_ge(s_qkvhi, 4 * a + 4)
                rows_ = slice(4 * half, 4 * half + 4)
                dve.tensor_tensor(out=v[:, 1, rows_, :].rearrange("p c d -> p (c d)"), in0=ps[:, VT_BANK[half], :],
                                  in1=f32(v[:, 0, rows_, :]).rearrange("p c d -> p (c d)"), op=ALU.subtract)\
                    .then_inc(s_qkvlo, 1)

            for b in range(2):
                a, t = 2 * b, 6 + 2 * b
                if b == 0:
                    x_lo(5)
                ln_stats(t, range(RT), XN_LOADS[t])
                ln_var(t)
                qk_lo(a, 0, qT)
                if b == 0:
                    ln_apply(t, range(RT))
                qk_lo(a, 1, kT)
                if b:
                    x_lo(5 + a, (2, 3))
                    ln_apply(t, range(RT))
                v_lo(a)
                a, t = 2 * b + 1, None if b else 7
                qk_lo(a, 1, kT)
                x_lo(5 + a)
                maximum(b, 0)
                maximum(b, 1)
                if t:
                    ln_stats(t, range(RT), XN_LOADS[t])
                p_lo(b, 0)
                qk_lo(a, 0, qT)
                p_lo(b, 1)
                v_lo(a)
                for g in range(QT // 2):
                    if g:
                        p_lo(b, 2 * g)
                    if g < 3:
                        maximum(b, 2 * g + 2)
                    if g:
                        p_lo(b, 2 * g + 1)
                    inverse(b, 2 * g)
                    inverse(b, 2 * g + 1)
                    if g < 3:
                        maximum(b, 2 * g + 3)
                    if t and g == 1:
                        ln_var(t)
                    if t and g == 3:
                        ln_apply(t, range(RT))
                    dve.wait_ge(s_ohi, 4 * b + g + 1)
                    dve.tensor_tensor(out=oT[:, g % 2, 1, :], in0=ps[:, PV_BANK, 0:2 * P], in1=f32(oT[:, g % 2, 0, :]),
                                      op=ALU.subtract).then_inc(s_olo, 1)
                if b:
                    total(1, QT - 2)
                    total(1, QT - 1)
                else:
                    x_lo(7, (0, 1))

            ffn_round(1, 0, BACK, True)
            with dve.Fori(1, ROUNDS - 1) as c:
                ffn_round(1, c, None, True)
            ffn_round(1, ROUNDS - 1, None, False)

        @block.gpsimd
        def _(pool):
            def deviation(t):
                pool.wait_ge(s_var, 2 * (t + 1))
                pool.tensor_tensor(out=rstd[:, :], in0=rstd[:, :], in1=mhalf[:, :], op=ALU.pow).then_inc(s_rstd, 1)

            def w_lo(item, u, src):
                pool.wait_ge(s_whi, item + 1)
                pool.tensor_tensor(out=unit_weights(u, 1), in0=unit_view(u, src), in1=f32(unit_weights(u, 0)),
                                   op=ALU.subtract).then_inc(s_wlo, 1)

            _, (sc_d, _, _, _, zq_d, _, _) = cuts
            pool.dma_start(sc_d, flat(scales[2], SC_D)).then_inc(d_cut_d, 16)
            pool.dma_start(zq_d, flat(zeros[2], ZC_D)).then_inc(d_cut_d, 16)
            for row, first in ((0, 0), (FOLD, D_FROM)):
                pool.dma_start(idx[row:row + FOLD, DOWN_COLS], spread(g_idx[2][first:first + D_COLS])).then_inc(d_idx_d, 16)
            pool.memset(mhalf[:, :], -0.5).then_inc(s_cst, 1)
            pool.wait_ge(s_cst, 1)
            parts = maker(pool, s_cut)
            pool.wait_ge(d_cut_gu, 64)
            cut_scales(pool, parts, *cuts[0])
            pool.wait_ge(d_cut_d, 32)
            cut_scales(pool, parts, *cuts[1])
            deviation(0)
            pool.wait_ge(d_grp, 16)
            pool.wait_ge(d_idx_d, 32)
            clamp_and_compare(pool, maker(pool, s_ohd), DOWN_COLS, GD, 1, oh_d[:, :])

            def ffn(phase):
                for u in range(SAVED if phase else 0, UNITS):
                    if u == 16:
                        deviation(8 * phase + 1)
                    if phase:
                        w_lo(ITEM_BACK + u - SAVED, u, wback[:, (u - SAVED) % WSLOTS, :])
                    else:
                        w_lo(u, u, wf[:, u % 2, :])
                with pool.Fori(1, ROUNDS - 1) as c:
                    deviation(8 * phase + 1 + c)

            ffn(0)
            for k in range(KT):
                pool.wait_ge(s_whi, ITEM_QKV + k + 1)
                pool.tensor_tensor(out=wq[:, 1, k, :], in0=wf[:, (ITEM_QKV + k) % 2, 0:3 * HEAD], in1=f32(wq[:, 0, k, :]),
                                   op=ALU.subtract).then_inc(s_wlo, 1)
            deviation(4)
            deviation(5)
            pool.wait_ge(s_whi, ITEM_O + 1)
            pool.tensor_tensor(out=wo[:, 1, :], in0=wf[:, ITEM_O % 2, :], in1=f32(wo[:, 0, :]), op=ALU.subtract).then_inc(s_wlo, 1)
            pool.wait_ge(d_bo, 16)

            def add_bias(b, tiles):
                for j in tiles:
                    r = j % RT
                    pool.wait_ge(d_res[r], 16 * (5 + 2 * b + j // RT))
                    pool.tensor_tensor(out=xres[:, r, :], in0=xres[:, r, :], in1=bo[:, :], op=ALU.add).then_inc(s_xb, 1)

            def total(b, j):
                pool.wait_ge(s_out, QT * b + j + 1)
                pool.tensor_tensor(out=xres[:, j % RT, :], in0=xres[:, j % RT, :], in1=osb[:, j % 2, :], op=ALU.add)\
                    .then_inc(s_att, 1)

            for b in range(2):
                deviation(6 + 2 * b)
                add_bias(b, range(RT))
                if b == 0:
                    deviation(7)
                for j in range(QT):
                    if not by_dve(b, j):
                        pool.wait_ge(s_xb, QT * b + j + 1)
                        total(b, j)
                    if 2 <= j <= RT + 1:
                        add_bias(b, [j - 2 + RT])
            ffn(1)


def kernel(**inputs):
    import concourse.bacc as bacc
    from concourse.bass_utils import run_bass_kernel_spmd

    nc = bacc.Bacc("TRN2", target_bir_lowering=False, num_devices=1)
    arrays = {}

    def take(name, a):
        a = np.ascontiguousarray(a)
        arrays[name] = a
        return nc.dram_tensor(name, a.shape, mybir.dt.from_np(a.dtype), kind="ExternalInput").ap()

    src = {k: take(f"in_{k}", np.asarray(v)) for k, v in inputs.items()}
    ident = take("in_ident", np.eye(P, dtype=np.float32))
    shifts = take("in_shifts", (BITS * (np.arange(P) % PACK)).astype(np.int32)[:, None])
    rows = np.arange(P) % FOLD
    group = np.stack([rows % GK, np.where(rows < Z_ROW, rows % GD, rows - Z_ROW)], 1)
    groups = take("in_groups", np.concatenate([group, group - [GK, GD]], 1).astype(np.float32))
    out = nc.dram_tensor("out_0", (TOKENS, HID), F32, kind="ExternalOutput").ap()
    mats = ("gate", "up", "down")
    macaron(nc, src["L0_attn_x"].rearrange("b s c -> (b s) c"), src["L0_attn_Wqkv"], src["L0_attn_bqkv"],
            src["L0_attn_Wo"], src["L0_attn_bo"], [src[f"L0_ffn_{m}_qweight"] for m in mats],
            [src[f"L0_ffn_{m}_scales"] for m in mats], [src[f"L0_ffn_{m}_qzeros"] for m in mats],
            [src[f"L0_ffn_{m}_g_idx"] for m in mats], ident, shifts, groups, out)
    r = run_bass_kernel_spmd(nc, [arrays], core_ids=[0])
    return r.results[0]["out_0"].reshape(inputs["L0_attn_x"].shape)
```
